# Optimizing a Trainium2 kernel written in Bass

```python
import numpy as np
import jax
import jax.numpy as jnp

def _softmax(x, axis=-1):
    return jax.nn.softmax(x, axis=axis)

def _gelu(x):
    return jax.nn.gelu(x, approximate=True)

def _silu(x):
    return jax.nn.silu(x)

def _sigmoid(x):
    return jax.nn.sigmoid(x)

def _layernorm(x, axis=-1, eps=1e-05):
    m = jnp.mean(x, axis=axis, keepdims=True)
    v = jnp.var(x, axis=axis, keepdims=True)
    return (x - m) / jnp.sqrt(v + eps)

def _scatter_add(tgt, idx, src, axis=0):
    return tgt.at[idx].add(src)

def _segment_sum(src, seg, n):
    return jax.ops.segment_sum(src, seg, n)
kernel_name = 'mk_gnn_preln_d2_gnn_r64_59b6d0'

def setup_inputs(seed: int=0):
    np.random.seed(seed)
    _w = jnp.asarray

    def _rec_inputs():
        import jax
        import jax.numpy as jnp
        _gk = jax.random.key(seed)
        x = -0.000202 + 1 * jax.random.normal(jax.random.fold_in(_gk, 1), (100000, 64), jnp.float32)
        src = jax.random.randint(jax.random.fold_in(_gk, 2), (50000,), 0, 100000, jnp.int32)
        dst = jax.random.randint(jax.random.fold_in(_gk, 3), (50000,), 0, 100000, jnp.int32)
        _o = jnp.argsort(dst, stable=True)
        src = src[_o]
        dst = dst[_o]
        edge_attr_32 = -5.16925e-05 + 1.00005 * jax.random.normal(jax.random.fold_in(_gk, 13), (50000, 32), jnp.float32)
        return (x, src, dst, edge_attr_32)
    x, src, dst, edge_attr_32 = _rec_inputs()

    def _L0_gnn_setup():
        import jax, jax.numpy as jnp
        import numpy as np
        N_NODES = 100000
        N_EDGES = 50000
        EDGE_OUT = 32
        HID = 128
        NODE_OUT = 64
        N_GRAPHS = 16
        key = jax.random.key(seed)
        ks = jax.random.split(key, 9)
        x = jax.random.normal(ks[0], (N_NODES, 64), dtype=jnp.float32)
        edge_index = jax.random.randint(ks[1], (2, N_EDGES), 0, N_NODES, dtype=jnp.int64)
        edge_attr = jax.random.normal(ks[2], (N_EDGES, EDGE_OUT), dtype=jnp.float32)
        u = jax.random.normal(ks[3], (N_GRAPHS, 1), dtype=jnp.float32)
        batch = jnp.sort(jax.random.randint(ks[4], (N_NODES,), 0, N_GRAPHS, dtype=jnp.int64))
        d_in = 3 * EDGE_OUT + 1
        W1 = jax.random.normal(ks[5], (d_in, HID), dtype=jnp.float32) / np.sqrt(d_in)
        b1 = jnp.zeros((HID,), dtype=jnp.float32)
        W2 = jax.random.normal(ks[6], (HID, NODE_OUT), dtype=jnp.float32) / np.sqrt(HID)
        b2 = jnp.zeros((NODE_OUT,), dtype=jnp.float32)
        return {'x': x, 'edge_index': edge_index, 'edge_attr': edge_attr, 'u': u, 'batch': batch, 'W1': W1, 'b1': b1, 'W2': W2, 'b2': b2}
    _L0_gnn_all = _L0_gnn_setup()
    _L0_gnn_in = {k: v for k, v in _L0_gnn_all.items() if k in ('u', 'W1', 'b1', 'W2', 'b2')}
    del _L0_gnn_all

    def _L1_gnn_setup():
        import jax, jax.numpy as jnp
        import numpy as np
        N_NODES = 100000
        key = jax.random.key(seed)
        k1, k2, k3, k4, k5 = jax.random.split(key, 5)
        feat = jax.random.normal(k1, (N_NODES, 64), dtype=jnp.float32)
        W = jax.random.normal(k2, (64, 64), dtype=jnp.float32) * 0.125
        b = jax.random.normal(k3, (64,), dtype=jnp.float32) * 0.01
        E = 25000
        src = jax.random.randint(k4, (E,), 0, N_NODES, dtype=jnp.int32)
        dst = jax.random.randint(k5, (E,), 0, N_NODES, dtype=jnp.int32)
        return {'feat': feat, 'W': W, 'b': b, 'src': src, 'dst': dst}
    _L1_gnn_all = _L1_gnn_setup()
    _L1_gnn_in = {k: v for k, v in _L1_gnn_all.items() if k in ('W', 'b')}
    del _L1_gnn_all
    return {'x': x, 'src': src, 'dst': dst, 'edge_attr_32': edge_attr_32, 'L0_gnn_u': _L0_gnn_in['u'], 'L0_gnn_W1': _L0_gnn_in['W1'], 'L0_gnn_b1': _L0_gnn_in['b1'], 'L0_gnn_W2': _L0_gnn_in['W2'], 'L0_gnn_b2': _L0_gnn_in['b2'], 'L1_gnn_W': _L1_gnn_in['W'], 'L1_gnn_b': _L1_gnn_in['b']}

def reference(x, src, dst, edge_attr_32, L0_gnn_u, L0_gnn_W1, L0_gnn_b1, L0_gnn_W2, L0_gnn_b2, L1_gnn_W, L1_gnn_b):
    import jax
    import jax.numpy as jnp

    def _L0_gnn_ref(x, edge_index, edge_attr, u, batch, W1, b1, W2, b2):
        import jax, jax.numpy as jnp
        import numpy as np
        N_NODES = 100000
        N_EDGES = 50000
        EDGE_OUT = 32
        HID = 128
        NODE_OUT = 64
        N_GRAPHS = 16
        N = x.shape[0]
        row = edge_index[0]
        seg_sum = jax.ops.segment_sum(edge_attr, row, num_segments=N)
        seg_max = jax.ops.segment_max(edge_attr, row, num_segments=N)
        cnt = jax.ops.segment_sum(jnp.ones((edge_attr.shape[0], 1), edge_attr.dtype), row, num_segments=N)
        seg_mean = seg_sum / jnp.maximum(cnt, 1.0)
        seg_max = jnp.where(cnt > 0, seg_max, 0.0)
        h = jnp.concatenate([seg_sum, seg_max, seg_mean, u[batch]], axis=1)
        h = jax.nn.relu(h @ W1 + b1)
        return h @ W2 + b2

    def _L1_gnn_ref(feat, W, b, src, dst):
        import jax, jax.numpy as jnp
        import numpy as np
        N_NODES = 100000
        agg = jax.ops.segment_sum(feat[src], dst, num_segments=feat.shape[0])
        h = agg @ W.T + b
        return jax.nn.relu(h)
    edge_index = jnp.stack([src, dst])
    batch0 = jnp.zeros((100000,), jnp.int32)
    h = jnp.maximum(_layernorm(x, axis=-1), 0.0)
    x = x + _L0_gnn_ref(h, edge_index, edge_attr_32, L0_gnn_u, batch0, L0_gnn_W1, L0_gnn_b1, L0_gnn_W2, L0_gnn_b2)
    h = jnp.maximum(_layernorm(x, axis=-1), 0.0)
    x = x + _L1_gnn_ref(h, L1_gnn_W, L1_gnn_b, src, dst)
    return x

_drawn_inputs = setup_inputs


def setup_inputs(seed=0):
    import zlib

    import numpy as np

    out = dict(_drawn_inputs(seed))
    spreads = {'L0_gnn_b1': (0.0, 0.1), 'L0_gnn_b2': (0.0, 0.1)}
    factors = {'L1_gnn_b': 8.0}
    for name, (base, spread) in spreads.items():
        noise = np.random.default_rng([zlib.crc32(name.encode()), seed]).standard_normal(out[name].shape)
        drawn = base * np.exp(spread * noise) if base else spread * noise
        out[name] = jnp.asarray(drawn.astype(out[name].dtype))
    for name, factor in factors.items():
        out[name] = (out[name] * factor).astype(out[name].dtype)
    return out
```

```python
from contextlib import ExitStack

import concourse.bass as bass
from concourse import mybir

F32 = mybir.dt.float32
I32 = mybir.dt.int32
U32 = mybir.dt.uint32
ALU = mybir.AluOpType
ACT = mybir.ActivationFunctionType
AX = mybir.AxisListType

P = 128
N = 100000
E = 50000
FE = 32
D = 64
HID = 128
EPS = 1e-5

COLS = 512
POS = P * COLS
BT = 4
BLK = BT * P
BLOCKS = -(-E // BLK)
LOOPS = BLOCKS // 2
DUMMY = 2 * BLK
ROWS = N + DUMMY
DR = 8
DENSE = P * DR * BLOCKS
HALF_E = E // 2
LOW = 15
SPLIT = 507 * P
BIG = 3.4028e38
assert BLOCKS % 2 == 0 and DENSE >= N and DENSE <= ROWS and HALF_E < 2 ** LOW


def build(nc, x, src, dst, edge_attr, u, W1, b1, W2, b2, W, b, out):
    T = nc.dram_tensor("node_table", [ROWS, D], F32).ap()
    line = nc.dram_tensor("node_line", [2, POS + 2], F32).ap()
    rows_src = nc.dram_tensor("rows_src", [3, POS], F32).ap()
    rows_dst = nc.dram_tensor("rows_dst", [1, POS], F32).ap()

    with ExitStack() as ctx:
        def sb(name, shape, dt=F32):
            return ctx.enter_context(nc.sbuf_tensor(name, shape, dt))

        def ps(name, shape):
            return ctx.enter_context(nc.psum_tensor(name, shape, F32))

        def sem(name):
            return ctx.enter_context(nc.semaphore(name))

        ident = sb("ident", [P, P])
        one = sb("one", [1, P])
        pos_i = sb("pos_i", [P, COLS], I32)
        pos_f = sb("pos_f", [P, COLS])
        low_i = sb("low_i", [P, COLS], I32)
        dummy_f = sb("dummy_f", [P, COLS])
        prow_i = sb("prow_i", [P, P], I32)
        bit_a = sb("bit_a", [P, P], I32)
        bit_b = sb("bit_b", [P, P], I32)
        flip = sb("flip", [P, 7, P])
        psign_i = sb("psign_i", [P, 1], I32)
        psign = sb("psign", [P, 1])
        eps_t = sb("eps_t", [P, 1])
        guard = sb("guard", [1, 2])
        w1_s = sb("w1_s", [96, HID])
        w1u = sb("w1u", [P, 1])
        b1_s = sb("b1_s", [P, 1])
        u_s = sb("u_s", [P, 1])
        w2_s = sb("w2_s", [P, D])
        b2_bc = sb("b2_bc", [P, D])
        w_s = sb("w_s", [D, D])
        b_bc = sb("b_bc", [P, D])
        wb_s = sb("wb_s", [D + 1, D])
        bias_z = sb("bias_z", [P, 1])
        r0 = sb("r0", [P, P])
        nc_row = sb("nc_row", [1, D])
        c_bc = sb("c_bc", [P, D])
        relub = sb("relub", [P, D])
        k_bc = sb("k_bc", [P, D])
        node_i = sb("node_i", [P, COLS], I32)
        srcs_i = sb("srcs_i", [P, COLS], I32)
        ka = sb("ka", [P, COLS])
        kb = sb("kb", [P, COLS])
        ha = sb("ha", [P, COLS])
        hb = sb("hb", [P, COLS])
        tm = sb("tm", [P, COLS])
        td = sb("td", [P, COLS])
        nodef = sb("nodef", [P, COLS])
        gidx_f = sb("gidx_f", [P, COLS])
        prev_f = sb("prev_f", [P, COLS])
        next_f = sb("next_f", [P, COLS])
        rowmax = sb("rowmax", [P, 1])
        pmax = sb("pmax", [1, P + 1])
        carry_p = sb("carry_p", [P, 1])
        gi = [sb(f"gi{s}", [P, COLS], I32) for s in range(2)]
        sx = [sb(f"sx{s}", [P, COLS], I32) for s in range(2)]
        stage_i = [sb(f"stage_i{b_}", [P, BT], I32) for b_ in range(2)]
        attr = [sb(f"attr{b_}", [P, BT, FE]) for b_ in range(2)]
        attr3 = [sb(f"attr3_{b_}", [P, BT, 3, FE]) for b_ in range(2)]
        c_rows = [sb(f"c_rows{b_}", [96, BLK]) for b_ in range(2)]
        k_rows = [sb(f"k_rows{b_}", [96, BLK]) for b_ in range(2)]
        feats = [sb(f"feats{b_}", [96, BLK]) for b_ in range(2)]
        carry = sb("carry", [96, 1])
        hid = [sb(f"hid{b_}", [P, BLK]) for b_ in range(2)]
        keep = sb("keep", [P, BT * BLOCKS, D])
        send = [sb(f"send{b_}", [P, BT, D]) for b_ in range(2)]
        send_i = [sb(f"send_i{b_}", [P, BT], I32) for b_ in range(2)]
        xg = [sb(f"xg{b_}", [P, BT, D]) for b_ in range(2)]
        x1 = [sb(f"x1_{b_}", [P, BT, D]) for b_ in range(2)]
        stat = [sb(f"stat{b_}", [P, BT, 6]) for b_ in range(2)]
        mv = [sb(f"mv{b_}", [P, BT, 2]) for b_ in range(2)]
        sd = [sb(f"sd{b_}", [P, BT]) for b_ in range(2)]
        rstd = [sb(f"rstd{b_}", [P, BT]) for b_ in range(2)]
        nmr = [sb(f"nmr{b_}", [P, BT]) for b_ in range(2)]
        hn = [sb(f"hn{b_}", [P, BT, D]) for b_ in range(2)]
        agg = [sb(f"agg{b_}", [D + 1, BLK]) for b_ in range(2)]
        dense = [sb(f"dense{b_}", [P, DR, D]) for b_ in range(2)]

        p_g = [ps(f"p_g{b_}", [P, BLK]) for b_ in range(2)]
        p_z = [ps(f"p_z{b_}", [P, BLK]) for b_ in range(2)]
        p_m = [ps(f"p_m{b_}", [P, BT, 128]) for b_ in range(2)]
        p_t = ps("p_t", [P, COLS])
        p_u = ps("p_u", [P, COLS])

        s_w = sem("weights_loaded")
        s_const = sem("constants_made")
        s_pool = sem("pool_step")
        s_v = sem("vector_step")
        s_src = sem("src_loaded")
        s_dstl = sem("dst_loaded")
        s_pad = sem("pads_set")
        s_T = sem("table_filled")
        s_tt = sem("to_turn")
        s_pt = sem("pe_turned")
        s_pw = sem("pe_weights")
        s_line = sem("line_ready")
        s_lw = sem("line_written")
        s_nb = sem("neighbours_loaded")
        s_row = sem("rows_ready")
        s_rw = sem("rows_written")
        s_idx = sem("indices_ready")
        s_wts = sem("weights_ready")
        pool_blocks = sem("pool_blocks")
        pe_blocks = sem("pe_blocks")
        s_r0 = sem("r0_ready")

        def two(name):
            return [sem(f"{name}{b_}") for b_ in range(2)]

        staged, gathered, rows_in = two("staged"), two("gathered"), two("rows_in")
        turned, feats_ok = two("turned"), two("feats_ok")
        tripled = two("tripled")
        z_ok, hid_ok, m_ok, kept = two("z_ok"), two("hid_ok"), two("m_ok"), two("kept")
        carried, summed, maxed = sem("carried"), sem("summed"), sem("maxed")
        send_ok, sent = two("send_ok"), two("sent")
        staged2, gathered2, rows2_in = two("staged2"), two("gathered2"), two("rows2_in")
        x1_ok, stat_ok, var_ok, sd_ok = two("x1_ok"), two("stat_ok"), two("var_ok"), two("sd_ok")
        rstd_ok, norm_ok, h_ok, ht_ok = two("rstd_ok"), two("norm_ok"), two("h_ok"), two("ht_ok")
        agg_ok, y_ok, kept2 = two("agg_ok"), two("y_ok"), two("kept2")
        d_in, d_ok, d_out = two("dense_in"), two("dense_ok"), two("dense_out")
        send2_ok, sent2 = two("send2_ok"), two("sent2")
        s_tail = sem("tail_filled")

        turn_from, moves = [], 9 * 10 // 2
        for k in range(10, 17):
            turn_from.append(moves % 2)
            moves += 1 + (k - 9)
            turn_from.append(moves % 2)
            moves += 9
        key_tiles = [kb, ka]
        sorted_in = key_tiles[moves % 2]
        block = ctx.enter_context(nc.Block())

        def node_of(c):
            return c.rearrange("(a n) -> a n", a=1)

        @block.sync
        def _(sp):
            sp.wait_ge(s_pad, 1)
            full = HALF_E // COLS
            for h in range(2):
                sp.dma_start(node_i[64 * h:64 * h + full, :],
                             src[h * HALF_E:h * HALF_E + full * COLS].rearrange("(p j) -> p j", j=COLS)).then_inc(s_src, 16)
                sp.dma_start(node_i[64 * h + full:64 * h + full + 1, 0:HALF_E - full * COLS],
                             node_of(src[h * HALF_E + full * COLS:(h + 1) * HALF_E])).then_inc(s_src, 16)
            sp.dma_start(w1_s[:, :], W1[0:96, :]).then_inc(s_w, 16)
            sp.dma_start(w1u[:, :], W1[96, :].rearrange("(p a) -> p a", a=1)).then_inc(s_w, 16)
            sp.dma_start(b1_s[:, :], b1.rearrange("(p a) -> p a", a=1)).then_inc(s_w, 16)
            sp.dma_start(u_s[:, :], u[0:1, 0].partition_broadcast(P)).then_inc(s_w, 16)
            sp.dma_start(w2_s[:, :], W2).then_inc(s_w, 16)
            sp.dma_start(b2_bc[:, :], b2.partition_broadcast(P)).then_inc(s_w, 16)
            sp.dma_start(w_s[:, :], W).then_inc(s_w, 16)
            sp.dma_start(b_bc[:, :], b.partition_broadcast(P)).then_inc(s_w, 16)
            sp.dma_start(wb_s[D:D + 1, :], node_of(b)).then_inc(s_w, 16)
            flat = x.rearrange("(a r) d -> a (r d)", a=16)
            sp.dma_start(T[0:N, :].rearrange("(a r) d -> a (r d)", a=16), flat).then_inc(s_T, 16)
            sp.dma_start(T[N:ROWS, :], x[0:DUMMY, :]).then_inc(s_T, 16)
            sp.dma_start(out[DENSE:ROWS, :], x[0:ROWS - DENSE, :]).then_inc(s_tail, 16)

            sp.wait_ge(s_const, 1)

            def neighbours(side):
                sp.wait_ge(s_line, side + 1)
                sp.dma_start(line[side, 1:POS + 1].rearrange("(p j) -> p j", j=COLS), nodef[:, :]).then_inc(s_lw, 16)
                sp.dma_start(line[side:side + 1, 0:1], guard[:, 0:1]).then_inc(s_lw, 16)
                sp.dma_start(line[side:side + 1, POS + 1:POS + 2], guard[:, 1:2]).then_inc(s_lw, 16)
                sp.wait_ge(s_lw, 48 * (side + 1))
                sp.dma_start(prev_f[:, :], line[side, 0:POS].rearrange("(p j) -> p j", j=COLS)).then_inc(s_nb, 16)
                sp.dma_start(next_f[:, :], line[side, 2:POS + 2].rearrange("(p j) -> p j", j=COLS)).then_inc(s_nb, 16)

            neighbours(0)
            sp.wait_ge(s_row, 3)
            for r, t in enumerate((tm, td, ha)):
                sp.dma_start(rows_src[r].rearrange("(p j) -> p j", j=COLS), t[:, :]).then_inc(s_rw, 16)
            sp.wait_ge(s_rw, 48)

            def load_rows(n, b_):
                at = bass.ds(BLK * n, BLK)
                sp.dma_start(c_rows[b_][0:96, :], rows_src[0, at].partition_broadcast(96)).then_inc(rows_in[b_], 16)
                sp.dma_start(k_rows[b_][32:64, :], rows_src[1, at].partition_broadcast(32)).then_inc(rows_in[b_], 16)
                sp.dma_start(k_rows[b_][64:96, :], rows_src[2, at].partition_broadcast(32)).then_inc(rows_in[b_], 16)

            load_rows(0, 0)
            load_rows(1, 1)
            with nc.sync.Fori(0, LOOPS - 1) as i:
                for b_ in range(2):
                    sp.wait_ge(feats_ok[b_], i + 1)
                    load_rows(2 * i + 2 + b_, b_)

            sp.wait_ge(s_pad, 2)
            full = E // COLS
            for t, a in ((node_i, dst), (srcs_i, src)):
                sp.dma_start(t[0:full, :], a[0:full * COLS].rearrange("(p j) -> p j", j=COLS)).then_inc(s_dstl, 16)
                sp.dma_start(t[full:full + 1, 0:E - full * COLS], node_of(a[full * COLS:E])).then_inc(s_dstl, 16)
            neighbours(1)
            sp.wait_ge(s_row, 4)
            sp.dma_start(rows_dst[0].rearrange("(p j) -> p j", j=COLS), tm[:, :]).then_inc(s_rw, 16)
            sp.wait_ge(s_rw, 64)

            t_dense = T[0:DENSE, :].rearrange("(p t r) d -> p t r d", p=P, r=DR)
            o_dense = out[0:DENSE, :].rearrange("(p t r) d -> p t r d", p=P, r=DR)

            def load_rows2(n, b_):
                sp.dma_start(c_rows[b_][0:D, :], rows_dst[0, bass.ds(BLK * n, BLK)].partition_broadcast(D)).then_inc(rows2_in[b_], 16)

            def load_dense(n, b_):
                sp.dma_start(dense[b_][:, :, :].rearrange("p r d -> p (r d)"), t_dense[:, bass.ds(n, 1), :, :].rearrange("p t r d -> p (t r d)")).then_inc(d_in[b_], 16)

            def store_dense(n, b_):
                sp.dma_start(o_dense[:, bass.ds(n, 1), :, :].rearrange("p t r d -> p (t r d)"), dense[b_][:, :, :].rearrange("p r d -> p (r d)")).then_inc(d_out[b_], 16)

            for b_ in range(2):
                sp.wait_ge(feats_ok[b_], LOOPS)
                load_rows2(b_, b_)
            for b_ in range(2):
                sp.wait_ge(sent[b_], 16 * BT * LOOPS)
            for b_ in range(2):
                load_dense(b_, b_)
            with nc.sync.Fori(0, LOOPS - 1) as i:
                for b_ in range(2):
                    sp.wait_ge(d_ok[b_], i + 1)
                    store_dense(2 * i + b_, b_)
                    sp.wait_ge(agg_ok[b_], i + 1)
                    load_rows2(2 * i + 2 + b_, b_)
                    sp.wait_ge(d_out[b_], 16 * (i + 1))
                    load_dense(2 * i + 2 + b_, b_)
            for b_ in range(2):
                sp.wait_ge(d_ok[b_], LOOPS)
                store_dense(BLOCKS - 2 + b_, b_)
            for b_ in range(2):
                sp.wait_ge(d_out[b_], 16 * LOOPS)
                sp.wait_ge(sent2[b_], 16 * BT * LOOPS)
            sp.wait_ge(s_tail, 16)

        @block.gpsimd
        def _(pool):
            step = [0]

            def link(ins):
                step[0] += 1
                ins.then_inc(s_pool, 1)
                pool.wait_ge(s_pool, step[0])

            link(nc.gpsimd.iota(pos_i[:, :], [[1, COLS]], base=0, channel_multiplier=COLS))
            link(nc.gpsimd.iota(psign_i[:, :], [[1, 1]], base=0, channel_multiplier=1))
            link(nc.gpsimd.iota(prow_i[:, :], [[1, P]], base=0, channel_multiplier=0))
            link(nc.gpsimd.memset(guard[:, :], -1.0))
            link(nc.gpsimd.memset(eps_t[:, :], EPS))
            link(nc.gpsimd.memset(one[:, :], 1.0))
            for b_ in range(2):
                link(nc.gpsimd.memset(agg[b_][D:D + 1, :], 1.0))
            link(nc.gpsimd.memset(ident[:, :], 0.0))
            nc.gpsimd.affine_select(out=ident[:, :], in_=ident[:, :], compare_op=ALU.not_equal, fill=1.0, base=0,
                                    pattern=[[-1, P]], channel_multiplier=1).then_inc(s_const, 1)

            pool.wait_ge(s_idx, 1)
            with nc.gpsimd.Fori(0, LOOPS) as i:
                for b_ in range(2):
                    pool.wait_ge(staged[b_], i + 1)
                    pool.sem_inc(pool_blocks, 1)
                    for t in range(BT):
                        nc.gpsimd.indirect_dma_start(
                            out=attr[b_][:, t, :], out_offset=None, in_=edge_attr,
                            in_offset=bass.IndirectOffsetOnAxis(ap=stage_i[b_][:, t:t + 1], axis=0)).then_inc(gathered[b_], 16)
            pool.wait_ge(s_T, 32)
            with nc.gpsimd.Fori(0, LOOPS) as i:
                for b_ in range(2):
                    pool.wait_ge(send_ok[b_], i + 1)
                    pool.sem_inc(pool_blocks, 1)
                    for t in range(BT):
                        nc.gpsimd.indirect_dma_start(
                            out=T, out_offset=bass.IndirectOffsetOnAxis(ap=send_i[b_][:, t:t + 1], axis=0),
                            in_=send[b_][:, t, :], in_offset=None, compute_op=ALU.add).then_inc(sent[b_], 16)
            for b_ in range(2):
                pool.wait_ge(sent[b_], 16 * BT * LOOPS)
            pool.wait_ge(s_idx, 2)
            with nc.gpsimd.Fori(0, LOOPS) as i:
                for b_ in range(2):
                    pool.wait_ge(staged2[b_], i + 1)
                    pool.sem_inc(pool_blocks, 1)
                    for t in range(BT):
                        nc.gpsimd.indirect_dma_start(
                            out=xg[b_][:, t, :], out_offset=None, in_=T,
                            in_offset=bass.IndirectOffsetOnAxis(ap=stage_i[b_][:, t:t + 1], axis=0)).then_inc(gathered2[b_], 16)
            pool.wait_ge(s_tail, 16)
            for b_ in range(2):
                pool.wait_ge(d_out[b_], 16 * LOOPS)
            with nc.gpsimd.Fori(0, LOOPS) as i:
                for b_ in range(2):
                    pool.wait_ge(send2_ok[b_], i + 1)
                    pool.sem_inc(pool_blocks, 1)
                    for t in range(BT):
                        nc.gpsimd.indirect_dma_start(
                            out=out, out_offset=bass.IndirectOffsetOnAxis(ap=send_i[b_][:, t:t + 1], axis=0),
                            in_=send[b_][:, t, :], in_offset=None, compute_op=ALU.add).then_inc(sent2[b_], 16)

        @block.scalar
        def _(act):
            act.wait_ge(s_wts, 1)

            def triple(i, b_):
                act.wait_ge(gathered[b_], 16 * BT * (i + 1))
                nc.scalar.copy(attr3[b_][:, :, :, :], attr[b_][:, :, :].unsqueeze(2).to_broadcast([P, BT, 3, FE])).then_inc(tripled[b_], 1)

            def hidden_and_rows(i, b_):
                act.wait_ge(z_ok[b_], i + 1)
                nc.scalar.activation(hid[b_][:, :], p_z[b_][:, :], ACT.Relu, bias=bias_z[:, :]).then_inc(hid_ok[b_], 1)
                act.wait_ge(m_ok[b_], i + 1)
                nc.scalar.copy(keep[:, bass.ds(BT * (2 * i + b_), BT), :], p_m[b_][:, :, 0:D]).then_inc(kept[b_], 1)

            triple(0, 0)
            with nc.scalar.Fori(0, LOOPS - 1) as i:
                triple(i, 1)
                hidden_and_rows(i, 0)
                triple(i + 1, 0)
                hidden_and_rows(i, 1)
            triple(LOOPS - 1, 1)
            hidden_and_rows(LOOPS - 1, 0)
            hidden_and_rows(LOOPS - 1, 1)


            def hand_over(n, b_, side, ok):
                nc.scalar.copy(send_i[b_][:, :], sx[side][:, bass.ds(BT * n, BT)])
                nc.scalar.copy(send[b_][:, :, :], keep[:, bass.ds(BT * n, BT), :]).then_inc(ok[b_], 1)

            def hand_all(side, ok, done):
                for b_ in range(2):
                    hand_over(b_, b_, side, ok)
                with nc.scalar.Fori(0, LOOPS - 1) as i:
                    for b_ in range(2):
                        act.wait_ge(done[b_], 16 * BT * (i + 1))
                        hand_over(2 * i + 2 + b_, b_, side, ok)

            for b_ in range(2):
                act.wait_ge(kept[b_], LOOPS)
            act.wait_ge(s_idx, 1)
            hand_all(0, send_ok, sent)
            with nc.scalar.Fori(0, LOOPS) as i:
                for b_ in range(2):
                    act.wait_ge(var_ok[b_], i + 1)
                    nc.scalar.activation(sd[b_][:, :], mv[b_][:, :, 1], ACT.Sqrt, bias=eps_t[:, :]).then_inc(sd_ok[b_], 1)
                    act.wait_ge(norm_ok[b_], i + 1)
                    for t in range(BT):
                        last = nc.scalar.activation(hn[b_][:, t, :], x1[b_][:, t, :], ACT.Relu,
                                                    bias=nmr[b_][:, t:t + 1], scale=rstd[b_][:, t:t + 1])
                    last.then_inc(h_ok[b_], 1)
            for b_ in range(2):
                act.wait_ge(kept2[b_], LOOPS)
                act.wait_ge(sent[b_], 16 * BT * LOOPS)
            act.wait_ge(s_idx, 2)
            hand_all(1, send2_ok, sent2)

        @block.vector
        def _(dve):
            step = [0]
            v = nc.vector

            def link(ins):
                step[0] += 1
                ins.then_inc(s_v, 1)
                dve.wait_ge(s_v, step[0])

            v.memset(node_i[:, :], N).then_inc(s_pad, 1)
            dve.wait_ge(s_pool, 3)
            v.tensor_copy(pos_f[:, :], pos_i[:, :])
            v.tensor_scalar(low_i[:, :], pos_i[:, :], 2 ** LOW - 1, None, ALU.bitwise_and)
            link(v.tensor_scalar(srcs_i[:, :], pos_i[:, :], DUMMY - 1, None, ALU.bitwise_and))
            link(v.tensor_scalar(dummy_f[:, :], srcs_i[:, :], float(N), None, ALU.add))
            link(v.tensor_scalar(psign_i[:, :], psign_i[:, :], 1, None, ALU.bitwise_and))
            link(v.tensor_scalar(psign[:, :], psign_i[:, :], -2.0, 1.0, ALU.mult, ALU.add))
            for m in range(7):
                link(v.tensor_scalar(bit_a[:, :], prow_i[:, :], m, 1, ALU.logical_shift_right, ALU.bitwise_and))
                if m < 6:
                    link(v.tensor_scalar(bit_b[:, :], prow_i[:, :], m + 1, 1, ALU.logical_shift_right, ALU.bitwise_and))
                    link(v.tensor_tensor(bit_a[:, :], bit_a[:, :], bit_b[:, :], ALU.bitwise_xor))
                else:
                    link(v.tensor_copy(bit_b[:, :], bit_a[:, :]))
                    for q in range(BT):
                        v.tensor_copy(ha[:, q * P:(q + 1) * P], bit_b[:, :])
                link(v.tensor_scalar(flip[:, m, :], bit_a[:, :], -2.0, 1.0, ALU.mult, ALU.add))
            dve.wait_ge(s_w, 144)
            link(v.scalar_tensor_tensor(bias_z[:, :], w1u[:, :], u_s[:, 0:1], b1_s[:, :], ALU.mult, ALU.add))
            v.tensor_scalar(r0[:, :], bias_z[:, :].to_broadcast([P, P]), 0.0, None, ALU.max).then_inc(s_r0, 1)
            v.tensor_scalar(relub[:, :], b_bc[:, :], 0.0, None, ALU.max)
            dve.wait_ge(s_pw, 1)
            v.tensor_scalar(nc_row[:, :], p_t[0:1, 0:D], -1.0, None, ALU.mult)
            v.tensor_copy(wb_s[0:D, :], p_u[0:D, 0:D])
            link(v.tensor_tensor(c_bc[:, :], p_t[:, 0:D], b2_bc[:, :], ALU.add))
            v.tensor_tensor(k_bc[:, :], c_bc[:, :], relub[:, :], ALU.add).then_inc(s_wts, 1)
            dve.wait_ge(s_src, 64)
            link(v.tensor_scalar(tm[:, :], node_i[:, :], float(SPLIT), float(2 ** 16 - SPLIT), ALU.is_ge, ALU.mult))
            link(v.scalar_tensor_tensor(td[:, :], node_i[:, :], 256.0, tm[:, :], ALU.add, ALU.add))
            link(v.tensor_copy(kb[:, :].bitcast(I32), td[:, :]))
            link(v.tensor_scalar(kb[:, :].bitcast(I32), kb[:, :].bitcast(I32), LOW, None, ALU.logical_shift_left))
            link(v.tensor_tensor(ka[:, :].bitcast(I32), kb[:, :].bitcast(I32), low_i[:, :], ALU.bitwise_or))
            link(v.tensor_scalar(kb[:, :], ka[:, :], psign[:, :], None, ALU.mult))

            keys = [kb, ka]
            half = [ha, hb]

            def pairs(tile, d):
                w = tile[:, :].rearrange("p (n t d) -> p n t d", t=2, d=d)
                return w[:, :, 0, :], w[:, :, 1, :]

            def mirror(tile, m):
                w = tile[:, :].rearrange("p (n m) -> p n m", m=m)
                return w[:, :, 0:m // 2], w[:, :, m // 2:m][:, :, ::-1]

            def finish(ins, last):
                if last:
                    ins.then_inc(s_tt, 1)
                else:
                    link(ins)

            def exchange(view, arg, of=None, last=False):
                lo, hi = view(keys[0] if of is None else of, arg)
                to_lo, to_hi = view(keys[1], arg)
                if of is not None:
                    link(v.tensor_copy(to_hi, hi))
                    hi = to_hi
                v.tensor_tensor(to_lo, lo, hi, ALU.max)
                finish(v.tensor_tensor(to_hi, lo, hi, ALU.min), last)
                keys.reverse()

            def exchange_halves(d, of=None, half_of=None, last=False):
                lo, hi = pairs(keys[0] if of is None else of, d)
                to_lo, to_hi = pairs(keys[1], d)
                hlo, hhi = pairs(half[0] if half_of is None else half_of, d)
                to_hlo, to_hhi = pairs(half[1], d)
                if of is not None:
                    v.tensor_copy(to_hi, hi)
                    link(v.tensor_copy(to_hhi, hhi))
                    hi, hhi = to_hi, to_hhi
                first, _ = pairs(tm, d)
                apart, _ = pairs(td, d)
                v.tensor_tensor(first, lo, hi, ALU.is_ge)
                link(v.tensor_tensor(apart, hlo, hhi, ALU.subtract))
                v.tensor_tensor(to_lo, lo, hi, ALU.max)
                v.tensor_tensor(to_hi, lo, hi, ALU.min)
                link(v.tensor_tensor(first, first, apart, ALU.mult))
                low_half = v.tensor_tensor(to_hlo, hhi, first, ALU.add)
                if of is not None:
                    link(low_half)
                finish(v.tensor_tensor(to_hhi, hlo, first, ALU.subtract), last)
                keys.reverse()
                half.reverse()

            for k in range(1, 10):
                exchange(mirror, 2 ** k)
                for q in range(k - 2, -1, -1):
                    exchange(pairs, 2 ** q, last=(k == 9 and q == 0))
            for k in range(10, 17):
                assert keys[0] is key_tiles[turn_from[2 * (k - 10)]]
                dve.wait_ge(s_pt, 2 * (k - 10) + 1)
                link(v.tensor_tensor(keys[1][:, :].rearrange("c (b p) -> c b p", p=P),
                                     p_t[:, :].rearrange("c (b p) -> c b p", p=P),
                                     flip[:, k - 10:k - 9, :].to_broadcast([P, BT, P]), ALU.mult))
                keys.reverse()
                for q in range(k - 10, -1, -1):
                    if k < 16:
                        exchange(pairs, 2 ** q, last=q == 0)
                    else:
                        exchange_halves(2 ** q, last=q == 0)
                assert keys[0] is key_tiles[turn_from[2 * (k - 10) + 1]]
                dve.wait_ge(s_pt, 2 * (k - 10) + 2)
                for q in range(8, -1, -1):
                    of = p_t if q == 8 else None
                    if k < 16:
                        exchange(pairs, 2 ** q, of=of, last=q == 0)
                    else:
                        exchange_halves(2 ** q, of=of, half_of=p_u if q == 8 else None)

            turned_n = [14]

            def prepare(side, ka, kb):
                dve.wait_ge(s_nb, 32 * (side + 1))
                if side:
                    dve.wait_ge(s_rw, 48)
                v.tensor_tensor(tm[:, :], nodef[:, :], prev_f[:, :], ALU.is_equal).then_inc(s_row, 1)
                dve.wait_ge(s_row, 1 + 3 * side)
                if side == 0:
                    link(v.tensor_scalar(td[:, :], tm[:, :], 2.0, -1.0, ALU.mult, ALU.add))
                    link(v.tensor_scalar(kb[:, :], tm[:, :], -1.0, 1.0, ALU.mult, ALU.add))
                    v.tensor_scalar(td[:, :], td[:, :], BIG, None, ALU.mult).then_inc(s_row, 1)
                    link(v.tensor_tensor(kb[:, :], kb[:, :], pos_f[:, :], ALU.mult))
                    v.reduce_max(rowmax[:, :], kb[:, :], AX.X).then_inc(s_tt, 1)
                    link(v.memset(pmax[:, 0:1], 0.0))
                    turned_n[0] += 1
                    dve.wait_ge(s_pt, turned_n[0])
                    link(v.tensor_copy(prev_f[0:1, 0:P], p_u[0:1, 0:P]))
                    v.tensor_tensor_scan(pmax[0:1, 1:P + 1], prev_f[0:1, 0:P], prev_f[0:1, 0:P], 0.0,
                                         ALU.max, ALU.max).then_inc(s_tt, 1)
                    turned_n[0] += 1
                    dve.wait_ge(s_pt, turned_n[0])
                    link(v.tensor_copy(carry_p[:, :], p_u[:, 256:257]))
                    link(v.tensor_tensor_scan(ka[:, :], kb[:, :], kb[:, :], carry_p[:, 0:1], ALU.max, ALU.max))
                    link(v.scalar_tensor_tensor(kb[:, :], ka[:, :], -1.0, pos_f[:, :], ALU.mult, ALU.add))
                    link(v.tensor_scalar(kb[:, :], kb[:, :], 1.0, None, ALU.add))
                    v.reciprocal(ha[:, :], kb[:, :]).then_inc(s_row, 1)
                    dve.wait_ge(s_row, 3)
                v.tensor_tensor(kb[:, :], nodef[:, :], next_f[:, :], ALU.not_equal)
                link(v.tensor_tensor(ka[:, :], nodef[:, :], dummy_f[:, :], ALU.subtract))
                link(v.tensor_tensor(ka[:, :], ka[:, :], kb[:, :], ALU.mult))
                v.tensor_tensor(ka[:, :], ka[:, :], dummy_f[:, :], ALU.add).then_inc(s_tt, 1)
                turned_n[0] += 1
                dve.wait_ge(s_pt, turned_n[0])
                for tile, turned_ in ((gi[side], p_t), (sx[side], p_u)):
                    last = v.tensor_copy(tile[:, :].rearrange("c (p b) -> c b p", b=BT),
                                         turned_[:, :].rearrange("c (b p) -> c b p", p=P))
                last.then_inc(s_idx, 1)

            srt, spare, hs = keys[0], keys[1], half[0]
            assert srt is sorted_in and hs is ha
            v.tensor_scalar(node_i[:, :].bitcast(U32), srt[:, :].bitcast(U32), LOW, None, ALU.logical_shift_right)
            link(v.tensor_scalar(srcs_i[:, :], srt[:, :].bitcast(I32), 2 ** LOW - 1, None, ALU.bitwise_and))
            v.tensor_scalar(tm[:, :], node_i[:, :], float(2 ** 16), float(2 ** 16 - SPLIT), ALU.is_ge, ALU.mult)
            link(v.scalar_tensor_tensor(td[:, :], hs[:, :], float(HALF_E), srcs_i[:, :], ALU.mult, ALU.add))
            v.scalar_tensor_tensor(nodef[:, :], node_i[:, :], 256.0, tm[:, :], ALU.subtract, ALU.subtract).then_inc(s_line, 1)
            link(v.tensor_scalar(gidx_f[:, :], td[:, :], float(E - 1), None, ALU.min))
            prepare(0, srt, spare)

            def stage(n, b_, side, ok):
                v.tensor_copy(stage_i[b_][:, :], gi[side][:, bass.ds(BT * n, BT)]).then_inc(ok[b_], 1)

            dve.wait_ge(s_idx, 1)
            for b_ in range(2):
                stage(b_, b_, 0, staged)
            v.memset(carry[:, :], 0.0).then_inc(carried, 1)
            with nc.vector.Fori(0, LOOPS) as i:
                for b_ in range(2):
                    n = 2 * i + b_
                    dve.wait_ge(turned[b_], i + 1)
                    stage(n + 2, b_, 0, staged)
                    dve.wait_ge(rows_in[b_], 48 * (i + 1))
                    dve.wait_ge(carried, n + 1)
                    f, c, k = feats[b_], c_rows[b_], k_rows[b_]
                    v.tensor_tensor_scan(f[0:96, :], c[0:96, :], p_g[b_][0:96, :], carry[0:96, 0:1],
                                         ALU.mult, ALU.add).then_inc(summed, 1)
                    dve.wait_ge(summed, n + 1)
                    v.tensor_tensor_scan(f[32:64, :], k[32:64, :], p_g[b_][32:64, :], carry[32:64, 0:1],
                                         ALU.min, ALU.max).then_inc(maxed, 1)
                    dve.wait_ge(maxed, n + 1)
                    v.tensor_copy(carry[:, :], f[:, BLK - 1:BLK]).then_inc(carried, 1)
                    dve.wait_ge(carried, n + 2)
                    v.tensor_tensor(f[64:96, :], f[64:96, :], k[64:96, :], ALU.mult).then_inc(feats_ok[b_], 1)

            v.memset(srcs_i[:, :], 0)
            v.memset(node_i[:, :], N).then_inc(s_pad, 1)
            dve.wait_ge(s_dstl, 64)
            v.tensor_copy(gidx_f[:, :], srcs_i[:, :])
            v.tensor_copy(nodef[:, :], node_i[:, :]).then_inc(s_line, 1)
            prepare(1, ka, kb)
            dve.wait_ge(s_idx, 2)
            for b_ in range(2):
                stage(b_, b_, 1, staged2)
            dve.wait_ge(s_wts, 1)

            def gather_side(i, b_):
                n = 2 * i + b_
                dve.wait_ge(gathered2[b_], 16 * BT * (i + 1))
                v.tensor_tensor(x1[b_][:, :, :], xg[b_][:, :, :],
                                c_bc[:, :].unsqueeze(1).to_broadcast([P, BT, D]), ALU.add).then_inc(x1_ok[b_], 1)
                stage(n + 2, b_, 1, staged2)
                dve.wait_ge(x1_ok[b_], i + 1)
                for t in range(BT):
                    last = v.bn_stats(stat[b_][:, t, :], x1[b_][:, t, :])
                last.then_inc(stat_ok[b_], 1)
                dve.wait_ge(stat_ok[b_], i + 1)
                dve.wait_ge(d_in[b_], 16 * (i + 1))
                v.tensor_tensor(dense[b_][:, :, :], dense[b_][:, :, :],
                                k_bc[:, :].unsqueeze(1).to_broadcast([P, DR, D]), ALU.add).then_inc(d_ok[b_], 1)
                for t in range(BT):
                    last = v.bn_aggr(mv[b_][:, t, :], stat[b_][:, t, :])
                last.then_inc(var_ok[b_], 1)

            def norm(i, b_):
                dve.wait_ge(sd_ok[b_], i + 1)
                v.reciprocal(rstd[b_][:, :], sd[b_][:, :]).then_inc(rstd_ok[b_], 1)
                dve.wait_ge(rstd_ok[b_], i + 1)
                v.scalar_tensor_tensor(nmr[b_][:, :], mv[b_][:, :, 0], -1.0, rstd[b_][:, :],
                                       ALU.mult, ALU.mult).then_inc(norm_ok[b_], 1)

            def scan2(i, b_, first=False):
                dve.wait_ge(ht_ok[b_], i + 1)
                dve.wait_ge(rows2_in[b_], 16 * (i + 1))
                if first:
                    before = 0.0
                else:
                    dve.wait_ge(agg_ok[1 - b_], i + b_)
                    before = agg[1 - b_][0:D, BLK - 1:BLK]
                v.tensor_tensor_scan(agg[b_][0:D, :], c_rows[b_][0:D, :], p_g[b_][0:D, :], before,
                                     ALU.mult, ALU.add).then_inc(agg_ok[b_], 1)

            def conv_out(i, b_):
                dve.wait_ge(y_ok[b_], i + 1)
                v.scalar_tensor_tensor(keep[:, bass.ds(BT * (2 * i + b_), BT), :], p_m[b_][:, :, 0:D], 0.0,
                                       relub[:, :].unsqueeze(1).to_broadcast([P, BT, D]),
                                       ALU.max, ALU.subtract).then_inc(kept2[b_], 1)

            for b_ in range(2):
                dve.wait_ge(send_ok[b_], LOOPS)
            gather_side(0, 0)
            norm(0, 0)
            gather_side(0, 1)
            scan2(0, 0, first=True)
            norm(0, 1)
            with nc.vector.Fori(1, LOOPS) as i:
                gather_side(i, 0)
                scan2(i - 1, 1)
                norm(i, 0)
                conv_out(i - 1, 0)
                gather_side(i, 1)
                scan2(i, 0)
                norm(i, 1)
                conv_out(i - 1, 1)
            scan2(LOOPS - 1, 1)
            conv_out(LOOPS - 1, 0)
            conv_out(LOOPS - 1, 1)

        @block.tensor
        def _(pe):
            mm = nc.tensor.matmul
            tr = nc.tensor.transpose
            pe.wait_ge(s_const, 1)
            pe.wait_ge(s_r0, 1)
            mm(p_t[:, 0:D], r0[:, :], w2_s[:, :], start=True, stop=True)
            tr(p_u[0:D, 0:D], w_s[:, :], ident[0:D, 0:D]).then_inc(s_pw, 1)
            pe.wait_ge(s_wts, 1)

            def turn(to, of):
                for q in range(BT):
                    last = tr(to[:, q * P:(q + 1) * P], of[:, q * P:(q + 1) * P], ident[:, :])
                return last

            for t, which in enumerate(turn_from):
                pe.wait_ge(s_tt, t + 1)
                last = turn(p_t, key_tiles[which])
                if t == 13:
                    last = turn(p_u, hb)
                last.then_inc(s_pt, 1)

            def rowmax_turns():
                pe.wait_ge(s_tt, 15)
                tr(p_u[0:1, 0:P], rowmax[:, :], ident[:, :]).then_inc(s_pt, 1)
                pe.wait_ge(s_tt, 16)
                mm(p_u[:, 256:257], pmax[0:1, 0:P], one[0:1, 0:1], start=True, stop=True).then_inc(s_pt, 1)

            rowmax_turns()
            pe.wait_ge(s_tt, 17)
            turn(p_t, gidx_f)
            turn(p_u, sorted_in).then_inc(s_pt, 1)

            def turn_attr(i, b_):
                pe.wait_ge(tripled[b_], i + 1)
                for t in range(BT):
                    last = tr(p_g[b_][0:96, t * P:(t + 1) * P],
                                  attr3[b_][:, t, :, :].rearrange("p a f -> p (a f)"), ident[:, :])
                last.then_inc(turned[b_], 1)

            def mlp(i, b_):
                pe.wait_ge(feats_ok[b_], i + 1)
                mm(p_z[b_][:, :], w1_s[:, :], feats[b_][:, :], start=True, stop=True).then_inc(z_ok[b_], 1)
                pe.wait_ge(hid_ok[b_], i + 1)
                for t in range(BT):
                    mm(p_m[b_][:, t, 0:D], hid[b_][:, t * P:(t + 1) * P], w2_s[:, :], start=True, stop=False)
                    last = mm(p_m[b_][:, t, 0:D], one[0:1, :], nc_row[0:1, :], start=False, stop=True)
                last.then_inc(m_ok[b_], 1)

            turn_attr(0, 0)
            with nc.tensor.Fori(0, LOOPS - 1) as i:
                turn_attr(i, 1)
                mlp(i, 0)
                turn_attr(i + 1, 0)
                mlp(i, 1)
            turn_attr(LOOPS - 1, 1)
            mlp(LOOPS - 1, 0)
            mlp(LOOPS - 1, 1)

            pe.wait_ge(s_tt, 18)
            turn(p_t, gidx_f)
            turn(p_u, ka).then_inc(s_pt, 1)

            def turn_h(i, b_):
                pe.wait_ge(h_ok[b_], i + 1)
                pe.sem_inc(pe_blocks, 1)
                for t in range(BT):
                    last = tr(p_g[b_][0:D, t * P:(t + 1) * P], hn[b_][:, t, :], ident[:, :])
                last.then_inc(ht_ok[b_], 1)

            def conv(i, b_):
                pe.wait_ge(agg_ok[b_], i + 1)
                for t in range(BT):
                    last = mm(p_m[b_][:, t, 0:D], agg[b_][:, t * P:(t + 1) * P], wb_s[:, :], start=True, stop=True)
                last.then_inc(y_ok[b_], 1)

            turn_h(0, 0)
            with nc.tensor.Fori(0, LOOPS - 1) as i:
                turn_h(i, 1)
                conv(i, 0)
                turn_h(i + 1, 0)
                conv(i, 1)
            turn_h(LOOPS - 1, 1)
            conv(LOOPS - 1, 0)
            conv(LOOPS - 1, 1)


_INS = ['x', 'src', 'dst', 'edge_attr_32', 'L0_gnn_u', 'L0_gnn_W1', 'L0_gnn_b1', 'L0_gnn_W2', 'L0_gnn_b2',
        'L1_gnn_W', 'L1_gnn_b']


def kernel(**inputs):
    import numpy as _np
    import concourse.bacc as _bacc
    from concourse import mybir as _mybir
    from concourse.bass_utils import run_bass_kernel_spmd as _run

    nc = _bacc.Bacc("TRN2", target_bir_lowering=False, num_devices=1)
    arrays, args = {}, []
    for name in _INS:
        a = _np.ascontiguousarray(inputs[name])
        arrays[f"in_{name}_dram"] = a
        args.append(nc.dram_tensor(f"in_{name}_dram", a.shape, _mybir.dt.from_np(a.dtype), kind="ExternalInput").ap())
    args.append(nc.dram_tensor("out_dram", (ROWS, D), _mybir.dt.float32, kind="ExternalOutput").ap())
    build(nc, *args)
    r = _run(nc, [arrays], core_ids=[0])
    return r.results[0]["out_dram"][:N]
```

```python
from contextlib import ExitStack

import concourse.bass as bass
from concourse import mybir

F32 = mybir.dt.float32
I32 = mybir.dt.int32
U32 = mybir.dt.uint32
BF16 = mybir.dt.bfloat16
F16 = mybir.dt.float16
ALU = mybir.AluOpType
ACT = mybir.ActivationFunctionType
AX = mybir.AxisListType


P = 128
N = 100000
E = 50000
FE = 32
D = 64
HID = 128
EPS = 1e-5

COLS = 512
POS = P * COLS
BT = 4
BLK = BT * P
BLOCKS = -(-E // BLK)
LOOPS = BLOCKS // 2
LAG = 8
GROUP = 512
STEP = 2 * GROUP
WROWS = 3 * P
REC = 66
WIDE = 1280
HIST = 32
PAD = 800 * P
DUMMY = 2 * BLK
ROWS = N + DUMMY
SPARE = ROWS - BLOCKS * STEP
HALF_E = E // 2
LOW = 15
SPLIT = 507 * P
LOW_TOP = SPLIT + 255
HIGH_ADD = 2 ** 16 + 256 - SPLIT
BIG = 3.4028e38
PIECE = 64
INNER = LAG // 2 + 2
assert SPARE % 96 == 0 and SPARE // 96 * D >= BT * REC and BLOCKS % 2 == 0 and BLOCKS * STEP >= N and BLOCKS * STEP <= ROWS
assert HALF_E < 2 ** LOW and LOW_TOP < 255 * 256 and PAD + HIGH_ADD < 2 ** 17


def back(i, b_, k):
    return i + (b_ - k) // 2, (b_ - k) % 2


def some(i, b_, k):
    return not isinstance(i, int) or 0 <= 2 * i + b_ - k < BLOCKS


def turns(eng, turn, start):
    for i in range(start, INNER):
        turn(i, 0)
        turn(i, 1)
    with eng.Fori(INNER, LOOPS - 1) as i:
        turn(i, 0)
        turn(i, 1)
    for i in range(LOOPS - 1, LOOPS + LAG // 2 + 2):
        turn(i, 0)
        turn(i, 1)


def build(nc, x, src, dst, edge_attr, u, W1, b1, W2, b2, W, b, out):
    T = nc.dram_tensor("node_table", [ROWS, D], F32).ap()
    line = nc.dram_tensor("node_line", [2, POS + 2], F32).ap()
    rows_src = nc.dram_tensor("rows_src", [4, POS], F32).ap()
    rows_dst = nc.dram_tensor("rows_dst", [1, POS], F32).ap()
    recs = [nc.dram_tensor(f"records{s}", [(BLOCKS + 1) * BLK, REC], F32).ap() for s in range(2)]
    starts = nc.dram_tensor("starts", [2, 200], I32).ap()

    with ExitStack() as ctx:
        def sb(name, shape, dt=F32):
            return ctx.enter_context(nc.sbuf_tensor(name, shape, dt))

        def ps(name, shape):
            return ctx.enter_context(nc.psum_tensor(name, shape, F32))

        def sem(name):
            return ctx.enter_context(nc.semaphore(name))

        def two(name):
            return [sem(f"{name}_{b_}") for b_ in range(2)]

        ident = sb("ident", [P, P])
        one = sb("one", [P, P])
        one_b = sb("one_b", [P, P], BF16)
        tri = sb("tri", [P, P])
        pos_i = sb("pos_i", [P, COLS], I32)
        pos_f = sb("pos_f", [P, COLS])
        low_i = sb("low_i", [P, COLS], I32)
        dummy_f = sb("dummy_f", [P, COLS])
        prow_i = sb("prow_i", [P, P], I32)
        bit_a = sb("bit_a", [P, P], I32)
        bit_b = sb("bit_b", [P, P], I32)
        flip = sb("flip", [P, 7, P])
        psign_i = sb("psign_i", [P, 1], I32)
        psign = sb("psign", [P, 1])
        eps_t = sb("eps_t", [P, 1])
        guard = sb("guard", [1, 2])
        count_b = sb("count_b", [P, HIST], BF16)
        node_i16 = sb("node_i16", [P, GROUP], I32)
        node_of = sb("node_of", [P, GROUP], F16)
        base_i = sb("base_i", [P, 2 * BLOCKS], I32)
        base_f = sb("base_f", [P, 2 * BLOCKS])
        limit_i = sb("limit_i", [P, 8], I32)
        limit = sb("limit", [P, 8])
        pad_rec = sb("pad_rec", [P, SPARE // 96 * D])
        w1_s = sb("w1_s", [96, HID])
        w1u = sb("w1u", [P, 1])
        b1_s = sb("b1_s", [P, 1])
        u_s = sb("u_s", [P, 1])
        w2_s = sb("w2_s", [P, D])
        b2_bc = sb("b2_bc", [P, D])
        w_s = sb("w_s", [D, D])
        b_bc = sb("b_bc", [P, D])
        wb_s = sb("wb_s", [D + 1, D])
        bias_z = sb("bias_z", [P, 1])
        r0 = sb("r0", [P, P])
        c_neg = sb("c_neg", [P, D])
        c3 = [sb(f"c3_{s}", [P, 2 * BT, D], BF16) for s in range(2)]
        nc3 = sb("nc3", [P, BT, D], BF16)
        part_b = [sb(f"part_b{q}", [P, D], BF16) for q in range(2)]
        part_f = [sb(f"part_f{q}", [P, D]) for q in range(3)]
        c_bc = sb("c_bc", [P, D])
        relub = sb("relub", [P, D])
        node_i = sb("node_i", [P, COLS], I32)
        srcs_i = sb("srcs_i", [P, COLS], I32)
        ka = sb("ka", [P, COLS])
        kb = sb("kb", [P, COLS])
        ha = sb("ha", [P, COLS])
        hb = sb("hb", [P, COLS])
        tm = sb("tm", [P, COLS])
        td = sb("td", [P, COLS])
        nodef = sb("nodef", [P, COLS])
        gidx_f = sb("gidx_f", [P, COLS])
        prev_f = sb("prev_f", [P, COLS])
        next_f = sb("next_f", [P, COLS])
        rowmax = sb("rowmax", [P, 1])
        pmax = sb("pmax", [1, P + 1])
        carry_p = sb("carry_p", [P, 1])
        dn_i = sb("dn_i", [P, COLS], I32)
        ds_i = sb("ds_i", [P, COLS], I32)
        dn_f = sb("dn_f", [P, COLS])
        ds_f = sb("ds_f", [P, COLS])
        pair = sb("pair", [P, 2], I32)
        gi = [sb(f"gi{s}", [P, COLS], I32) for s in range(2)]
        share = sb("share", [P, COLS])
        sx = sb("sx", [P, COLS], I32)
        rn = [sb(f"rn{s}", [P, COLS]) for s in range(2)]
        hi_i = sb("hi_i", [P, COLS], I32)
        lo_i = sb("lo_i", [P, COLS], I32)
        hi_b = sb("hi_b", [P, COLS], BF16)
        lo_b = sb("lo_b", [P, COLS], BF16)
        hi_oh = [sb(f"hi_oh{b_}", [P, PIECE, HIST], BF16) for b_ in range(2)]
        lo_oh = [sb(f"lo_oh{b_}", [P, PIECE, HIST], BF16) for b_ in range(2)]
        cnt = sb("cnt", [HIST, HIST])
        inc = sb("inc", [HIST, HIST])
        zero = sb("zero", [HIST, HIST])
        below = sb("below", [HIST, HIST + 1])
        over = sb("over", [HIST, 8])
        over2 = sb("over2", [HIST, 8])
        first_i = [sb(f"first_i{s}", [HIST, 8], I32) for s in range(2)]
        start_row = [sb(f"start_row{s}", [1, 200], I32) for s in range(2)]
        wrong = sb("wrong", [P, 4])
        wrong1 = sb("wrong1", [P, 1])
        fast = sb("fast", [1, 1], I32)
        stage_i = [sb(f"stage_i{b_}", [P, BT], I32) for b_ in range(2)]
        source_i = sb("source_i", [P, BT], I32)
        attr = [sb(f"attr{b_}", [P, BT, FE]) for b_ in range(2)]
        attr3 = [sb(f"attr3_{b_}", [P, BT, 3, FE]) for b_ in range(2)]
        c_rows = [sb(f"c_rows{b_}", [P, BLK]) for b_ in range(2)]
        feats = [sb(f"feats{b_}", [96, BLK]) for b_ in range(2)]
        carry = sb("carry", [96, 1])
        hid = [sb(f"hid{b_}", [P, BLK]) for b_ in range(2)]
        rec = [sb(f"rec{b_}", [P, BT, REC]) for b_ in range(2)]
        win = [sb(f"win{b_}", [P, 2, 3, REC]) for b_ in range(2)]
        rel = [sb(f"rel{b_}", [P, 2, 3]) for b_ in range(2)]
        oneh = [sb(f"oneh{b_}", [P, 2, WIDE], BF16) for b_ in range(2)]
        upper_b = [sb(f"upper_b{b_}", [P, 2, 3, D], BF16) for b_ in range(2)]
        rest = [sb(f"rest{b_}", [P, 2, 3, D]) for b_ in range(2)]
        lower_b = [sb(f"lower_b{b_}", [P, 2, 3, D], BF16) for b_ in range(2)]
        din = [sb(f"din{b_}", [P, 2 * BT * D]) for b_ in range(2)]
        dout = [sb(f"dout{b_}", [P, 2 * BT * D]) for b_ in range(2)]
        send_i = [sb(f"send_i{b_}", [P, BT], I32) for b_ in range(2)]
        xg = [sb(f"xg{b_}", [P, BT, D]) for b_ in range(2)]
        x1 = [sb(f"x1_{b_}", [P, BT, D]) for b_ in range(2)]
        stat = [sb(f"stat{b_}", [P, BT, 6]) for b_ in range(2)]
        mv = [sb(f"mv{b_}", [P, BT, 2]) for b_ in range(2)]
        sd = [sb(f"sd{b_}", [P, BT]) for b_ in range(2)]
        rstd = [sb(f"rstd{b_}", [P, BT]) for b_ in range(2)]
        nmr = [sb(f"nmr{b_}", [P, BT]) for b_ in range(2)]
        hn = [sb(f"hn{b_}", [P, BT, D]) for b_ in range(2)]
        agg = [sb(f"agg{b_}", [D + 1, BLK]) for b_ in range(2)]

        p_g = [ps(f"p_g{b_}", [P, BLK]) for b_ in range(2)]
        p_z = [ps(f"p_z{b_}", [P, BLK]) for b_ in range(2)]
        p_m = [ps(f"p_m{b_}", [P, BT, P]) for b_ in range(2)]
        p_t = ps("p_t", [P, COLS])
        p_u = ps("p_u", [P, COLS])
        p_e = [p_t, p_u]
        p_h = p_m[1]

        s_w = sem("weights_loaded")
        s_const = sem("constants_made")
        s_pool = sem("pool_step")
        s_v = sem("vector_step")
        s_src = sem("src_loaded")
        s_pad = sem("pads_set")
        s_dpad = sem("dst_pads_set")
        s_dstl = sem("dst_loaded")
        s_dplane = sem("dst_planes")
        s_dturn = sem("dst_turned")
        s_dcols = sem("dst_columns")
        s_oh = [sem(f"hist_onehot{s}") for s in range(2)]
        s_ohu = [sem(f"hist_used{s}") for s in range(2)]
        s_inc = sem("hist_scanned")
        s_base = sem("hist_base")
        s_wrong = sem("wrong_counted")
        s_wsum = sem("wrong_summed")
        s_first = sem("starts_made")
        s_fout = sem("starts_written")
        s_fin = sem("starts_loaded")
        s_fast = sem("choice_made")
        s_cplane = sem("count_planes")
        table_ok = sem("table_ok")
        s_tail = sem("tail_filled")
        s_tt = two("to_turn")
        s_pt = two("pe_turned")
        s_pw = sem("pe_weights")
        s_line = sem("line_ready")
        s_lw = sem("line_written")
        s_nb = sem("neighbours_loaded")
        s_row = sem("rows_ready")
        s_rw = sem("rows_written")
        s_idx = sem("indices_ready")
        s_wts = sem("weights_ready")
        pool_blocks = sem("pool_blocks")
        pe_blocks = sem("pe_blocks")
        sp_steps = sem("sp_steps")
        s_r0 = sem("r0_ready")

        staged, gathered, rows_in = two("staged"), two("gathered"), two("rows_in")
        tripled, turned, feats_ok = two("tripled"), two("turned"), two("feats_ok")
        z_ok, hid_ok, m_ok = two("z_ok"), two("hid_ok"), two("m_ok")
        carried, summed = sem("carried"), sem("summed")
        rec_ok = [two(f"rec_ok{s}") for s in range(2)]
        rec_out = [two(f"rec_out{s}") for s in range(2)]
        win_in = [two(f"win_in{s}") for s in range(2)]
        d_in = [two(f"dense_in{s}") for s in range(2)]
        rel_ok = [two(f"rel_ok{s}") for s in range(2)]
        hi_ok = [two(f"upper_part_ok{s}") for s in range(2)]
        rest_ok = [two(f"rest_ok{s}") for s in range(2)]
        lo_ok = [two(f"lower_part_ok{s}") for s in range(2)]
        exp_ok = [two(f"expanded{s}") for s in range(2)]
        sum_ok = [two(f"added{s}") for s in range(2)]
        d_out = [two(f"dense_out{s}") for s in range(2)]
        staged2, gathered2, copied = two("staged2"), two("gathered2"), two("copied")
        stat_ok, var_ok, sd_ok = two("stat_ok"), two("var_ok"), two("sd_ok")
        rstd_ok, norm_ok, h_ok, ht_ok = two("rstd_ok"), two("norm_ok"), two("h_ok"), two("ht_ok")
        hts_ok, y_ok = two("hts_ok"), two("y_ok")

        g_dense_in, g_dense_ok, g_dense_out = d_in[0], sum_ok[0], d_out[0]
        g_row_in, g_row_ok, g_sent = win_in[0], rel_ok[0], exp_ok[0]
        g_pad, g_dst_in, g_rows_stored = rel_ok[1][0], win_in[1][0], win_in[1][1]
        g_edge, g_source, g_x = staged2[0], gathered2[0], gathered2[1]
        g_stat, g_var, g_sd = stat_ok[0], var_ok[0], sd_ok[0]
        g_rstd, g_norm, g_h, g_ht = rstd_ok[0], norm_ok[0], h_ok[0], ht_ok[0]
        g_c, g_agg, g_carry = d_in[1][0], hts_ok[0], hts_ok[1]
        g_y, g_rec, g_stored = y_ok[0], rec_ok[1][0], rec_out[1][0]

        turn_from, moves = [], 9 * 10 // 2
        for k in range(10, 17):
            turn_from.append(moves % 2)
            moves += 1 + (k - 9)
            turn_from.append(moves % 2)
            moves += 9
        key_tiles = [kb, ka]
        sorted_in, spare = key_tiles[moves % 2], key_tiles[1 - moves % 2]
        block = ctx.enter_context(nc.Block())

        def as_row(c):
            return c.rearrange("(a n) -> a n", a=1)

        def as_rows(c):
            return c.rearrange("(p j) -> p j", j=COLS)

        def middle_of(b_):
            words = rest[b_][:, :, :, :].rearrange("p g a d -> p (g a d)").bitcast(BF16)
            return words.rearrange("p (g a d w) -> p g a d w", g=2, a=3, w=2)[:, :, :, :, 1]

        def dense_rows(table, m):
            return table[bass.ds(STEP * m, STEP), :].rearrange("(q p t) d -> p q (t d)", q=4, t=2)

        def buf_rows(tile):
            return tile[:, :].rearrange("p (q r) -> p q r", q=4)

        @block.sync
        def _(sp):
            sp.wait_ge(s_pad, 1)
            full = HALF_E // COLS
            for h in range(2):
                sp.dma_start(node_i[64 * h:64 * h + full, :],
                             as_rows(src[h * HALF_E:h * HALF_E + full * COLS])).then_inc(s_src, 16)
                sp.dma_start(node_i[64 * h + full:64 * h + full + 1, 0:HALF_E - full * COLS],
                             as_row(src[h * HALF_E + full * COLS:(h + 1) * HALF_E])).then_inc(s_src, 16)
            sp.dma_start(w1_s[:, :], W1[0:96, :]).then_inc(s_w, 16)
            sp.dma_start(w1u[:, :], W1[96, :].rearrange("(p a) -> p a", a=1)).then_inc(s_w, 16)
            sp.dma_start(b1_s[:, :], b1.rearrange("(p a) -> p a", a=1)).then_inc(s_w, 16)
            sp.dma_start(u_s[:, :], u[0:1, 0].partition_broadcast(P)).then_inc(s_w, 16)
            sp.dma_start(w2_s[:, :], W2).then_inc(s_w, 16)
            sp.dma_start(b2_bc[:, :], b2.partition_broadcast(P)).then_inc(s_w, 16)
            sp.dma_start(w_s[:, :], W).then_inc(s_w, 16)
            sp.dma_start(b_bc[:, :], b.partition_broadcast(P)).then_inc(s_w, 16)
            sp.dma_start(wb_s[D:D + 1, :], as_row(b)).then_inc(s_w, 16)
            sp.wait_ge(s_dpad, 1)
            full = E // COLS
            for t, a in ((dn_i, dst), (ds_i, src)):
                sp.dma_start(t[0:full, :], as_rows(a[0:full * COLS])).then_inc(s_dstl, 16)
                sp.dma_start(t[full:full + 1, 0:E - full * COLS], as_row(a[full * COLS:E])).then_inc(s_dstl, 16)
            sp.dma_start(pair[0:full - 1, :], as_rows(dst[COLS - 1:COLS - 1 + (full - 1) * COLS])[:, 0:2]).then_inc(s_dstl, 16)
            sp.dma_start(pair[full - 1:full, :], as_row(dst[full * COLS - 1:full * COLS + 1])).then_inc(s_dstl, 16)
            sp.wait_ge(s_const, 1)
            for s in range(2):
                sp.dma_start(recs[s][BLOCKS * BLK:, :].rearrange("(p t) r -> p (t r)", t=BT), pad_rec[:, 0:BT * REC]).then_inc(s_tail, 16)
            for t in (T, out):
                sp.dma_start(t[BLOCKS * STEP:ROWS, :].rearrange("(p c) d -> p (c d)", c=SPARE // 96), pad_rec[0:96, 0:SPARE // 96 * D]).then_inc(s_tail, 16)

            def neighbours(side):
                sp.wait_ge(s_line, side + 1)
                sp.dma_start(as_rows(line[side, 1:POS + 1]), nodef[:, :]).then_inc(s_lw, 16)
                sp.dma_start(line[side:side + 1, 0:1], guard[:, 0:1]).then_inc(s_lw, 16)
                sp.dma_start(line[side:side + 1, POS + 1:POS + 2], guard[:, 1:2]).then_inc(s_lw, 16)
                sp.wait_ge(s_lw, 48 * (side + 1))
                sp.dma_start(prev_f[:, :], as_rows(line[side, 0:POS])).then_inc(s_nb, 16)
                sp.dma_start(next_f[:, :], as_rows(line[side, 2:POS + 2])).then_inc(s_nb, 16)

            neighbours(0)
            sp.wait_ge(s_row, 3)
            for r, t in enumerate((tm, tm, hb, td)):
                sp.dma_start(as_rows(rows_src[r]), t[:, :]).then_inc(s_rw, 16)
            sp.wait_ge(s_rw, 64)

            def load_rows(n, b_):
                at = bass.ds(BLK * n, BLK)
                sp.dma_start(c_rows[b_][:, :], rows_src[:, at].unsqueeze(1).to_broadcast([4, FE, BLK])).then_inc(rows_in[b_], 16)

            def next_rows(i, b_):
                sp.wait_ge(feats_ok[b_], i + 1)
                load_rows(2 * i + 2 + b_, b_)

            def store_rec(side, i, b_):
                sp.wait_ge(rec_ok[side][b_], i + 1)
                sp.dma_start(recs[side][bass.ds(BLK * (2 * i + b_), BLK), :].rearrange("(p t) r -> p (t r)", t=BT),
                             rec[b_][:, :, :].rearrange("p t r -> p (t r)")).then_inc(rec_out[side][b_], 16)

            def window(side, j, b_):
                m = 2 * j + b_
                at = [sp.value_load(start_row[side][0:1, bass.ds(2 * m + g, 1)], min_val=0, max_val=E) for g in range(2)]
                stored = [(r_, 16 * (min(c, LOOPS - 1) + 1 if isinstance(c, int) else c + 1))
                          for c, r_ in (back(j, b_, -1), back(j, b_, -2))]
                for r_, count in stored:
                    sp.wait_ge(rec_out[side][r_], count)
                    sp.sem_inc(sp_steps, 1)
                if not isinstance(j, int) or j > 0:
                    sp.wait_ge(rest_ok[side][b_], j)
                for g in range(2):
                    sp.dma_start(win[b_][:, g, :, :], recs[side][bass.ds(at[g], WROWS), :].rearrange("(a p) r -> p a r", p=P)).then_inc(win_in[side][b_], 16)

            def load_dense(side, j, b_, table):
                if not isinstance(j, int) or j > 0:
                    sp.wait_ge(sum_ok[side][b_], j)
                if table is x and isinstance(j, int) and 2 * j + b_ == BLOCKS - 1:
                    left = N - (BLOCKS - 1) * STEP - GROUP
                    sp.dma_start(buf_rows(din[b_])[:, 0:2], x[N - left - GROUP:N - left, :].rearrange("(q p t) d -> p q (t d)", q=2, t=2)).then_inc(d_in[side][b_], 16)
                    sp.dma_start(buf_rows(din[b_])[0:left // 2, 2], x[N - left:N, :].rearrange("(p t) d -> p (t d)", t=2)).then_inc(d_in[side][b_], 16)
                else:
                    sp.dma_start(buf_rows(din[b_]), dense_rows(table, 2 * j + b_)).then_inc(d_in[side][b_], 16)

            def store_dense(side, j, b_, table):
                sp.wait_ge(sum_ok[side][b_], j + 1)
                sp.dma_start(dense_rows(table, 2 * j + b_), buf_rows(dout[b_])).then_inc(d_out[side][b_], 16)

            def turn_src(i, b_, expand=True):
                if expand and some(i, b_, LAG - 1):
                    window(0, *back(i, b_, LAG - 1))
                if some(i, b_, -2):
                    next_rows(i, b_)
                if some(i, b_, 1):
                    store_rec(0, *back(i, b_, 1))
                if expand and some(i, b_, LAG + 1):
                    load_dense(0, *back(i, b_, LAG + 1), x)
                if expand and some(i, b_, LAG + 3):
                    store_dense(0, *back(i, b_, LAG + 3), T)

            def turn_dst(i, b_, expand=True):
                if expand and some(i, b_, LAG - 1):
                    window(1, *back(i, b_, LAG - 1))
                if some(i, b_, 3):
                    store_rec(1, *back(i, b_, 3))
                if expand and some(i, b_, LAG + 1):
                    load_dense(1, *back(i, b_, LAG + 1), T)
                if expand and some(i, b_, LAG + 3):
                    store_dense(1, *back(i, b_, LAG + 3), out)

            load_rows(0, 0)
            load_rows(1, 1)
            for n in range(LAG - 1):
                turn_src(n // 2, n % 2)
            for s in range(2):
                sp.wait_ge(s_first, 2 - s)
                sp.dma_start(starts[s].rearrange("(p c) -> p c", c=8), first_i[s][0:25, :]).then_inc(s_fout, 16)
            sp.wait_ge(s_fout, 32)
            for s in range(2):
                sp.dma_start(start_row[s][:, :], starts[s:s + 1, :]).then_inc(s_fin, 16)
            sp.wait_ge(s_fin, 32)
            sp.wait_ge(s_tail, 64)
            sp.wait_ge(s_fast, 1)
            with sp.If(sp.value_load(fast[0:1, 0:1], min_val=0, max_val=1)):
                turn_src(LAG // 2 - 1, 1)
                turns(sp, turn_src, LAG // 2)
                for b_ in range(2):
                    sp.wait_ge(d_out[0][b_], 16 * LOOPS)
                sp.sem_inc(table_ok, 1)
                turns(sp, turn_dst, 0)
                for b_ in range(2):
                    sp.wait_ge(d_out[1][b_], 16 * LOOPS)
            with sp.Else():
                turn_src(LAG // 2 - 1, 1, expand=False)
                turns(sp, lambda i, b_: turn_src(i, b_, expand=False), LAG // 2)
                for b_ in range(2):
                    sp.wait_ge(rec_out[0][b_], 16 * LOOPS)

                def dense(side, table, to):
                    def step(n):
                        if table is x and isinstance(n, int):
                            left = N - (BLOCKS - 1) * STEP - GROUP
                            sp.dma_start(buf_rows(din[0])[:, 0:2], x[N - left - GROUP:N - left, :].rearrange("(q p t) d -> p q (t d)", q=2, t=2)).then_inc(g_dense_in[side], 16)
                            sp.dma_start(buf_rows(din[0])[0:left // 2, 2], x[N - left:N, :].rearrange("(p t) d -> p (t d)", t=2)).then_inc(g_dense_in[side], 16)
                        else:
                            sp.dma_start(buf_rows(din[0]), dense_rows(table, n)).then_inc(g_dense_in[side], 16)
                        sp.wait_ge(g_dense_ok[side], n + 1)
                        sp.dma_start(dense_rows(to, n), buf_rows(dout[0])).then_inc(g_dense_out[side], 16)
                        sp.wait_ge(g_dense_out[side], 16 * (n + 1))
                        sp.sem_inc(sp_steps, 1)

                    with nc.sync.Fori(0, BLOCKS - 1) as n:
                        step(n)
                    step(BLOCKS - 1)

                def load_records(side):
                    with nc.sync.Fori(0, BLOCKS) as n:
                        sp.dma_start(rec[0][:, :, :].rearrange("p t r -> p (t r)"),
                                     recs[side][bass.ds(BLK * n, BLK), :].rearrange("(p t) r -> p (t r)", t=BT)).then_inc(g_row_in[side], 16)
                        sp.wait_ge(g_sent[side], 16 * BT * (n + 1))
                        sp.sem_inc(sp_steps, 1)

                dense(0, x, T)
                load_records(0)
                sp.wait_ge(g_pad, 1)
                full = HALF_E // COLS
                for h in range(2):
                    sp.dma_start(node_i[64 * h:64 * h + full, :],
                                 as_rows(dst[h * HALF_E:h * HALF_E + full * COLS])).then_inc(g_dst_in, 16)
                    sp.dma_start(node_i[64 * h + full:64 * h + full + 1, 0:HALF_E - full * COLS],
                                 as_row(dst[h * HALF_E + full * COLS:(h + 1) * HALF_E])).then_inc(g_dst_in, 16)
                neighbours(1)
                sp.wait_ge(s_row, 4)
                sp.dma_start(as_rows(rows_dst[0]), tm[:, :]).then_inc(g_rows_stored, 16)
                sp.wait_ge(g_rows_stored, 16)
                dense(1, T, out)
                with nc.sync.Fori(0, BLOCKS) as n:
                    sp.dma_start(c_rows[0][0:D, :], rows_dst[0, bass.ds(BLK * n, BLK)].partition_broadcast(D)).then_inc(g_c, 16)
                    sp.wait_ge(g_rec, n + 1)
                    sp.dma_start(recs[1][bass.ds(BLK * n, BLK), :].rearrange("(p t) r -> p (t r)", t=BT),
                                 rec[0][:, :, :].rearrange("p t r -> p (t r)")).then_inc(g_stored, 16)
                    sp.wait_ge(g_stored, 16 * (n + 1))
                    sp.sem_inc(sp_steps, 1)
                load_records(1)

        @block.gpsimd
        def _(pool):
            g = nc.gpsimd
            step = [0]

            def link(ins):
                step[0] += 1
                ins.then_inc(s_pool, 1)
                pool.wait_ge(s_pool, step[0])

            link(g.iota(pos_i[:, :], [[1, COLS]], base=0, channel_multiplier=COLS))
            link(g.iota(psign_i[:, :], [[1, 1]], base=0, channel_multiplier=1))
            link(g.iota(prow_i[:, :], [[1, P]], base=0, channel_multiplier=0))
            link(g.memset(dn_i[:, :], PAD))
            g.memset(ds_i[:, :], 0).then_inc(s_dpad, 1)
            pool.wait_ge(s_dpad, 1)
            link(g.iota(node_i16[:, :], [[2 * P, 2], [1, 2], [2, P]], base=0, channel_multiplier=0))
            link(g.iota(base_i[:, :], [[GROUP, 2 * BLOCKS]], base=0, channel_multiplier=0))
            link(g.iota(limit_i[:, :], [[BLK, 4], [0, 2]], base=3 * BLK, channel_multiplier=4 * BLK))
            link(g.tensor_copy(node_of[:, :], node_i16[:, :]))
            link(g.tensor_copy(base_f[:, :], base_i[:, :]))
            link(g.tensor_copy(limit[:, :], limit_i[:, :]))
            link(g.tensor_copy(count_b[:, :], prow_i[:, 0:HIST]))
            link(g.memset(guard[:, :], -1.0))
            link(g.memset(eps_t[:, :], EPS))
            link(g.memset(one[:, :], 1.0))
            link(g.memset(one_b[:, :], 1.0))
            link(g.memset(zero[:, :], 0.0))
            link(g.memset(wrong[:, :], 0.0))
            link(g.memset(pad_rec[:, :], -1.0))
            for b_ in range(2):
                link(g.memset(agg[b_][D:D + 1, :], 1.0))
                link(g.memset(rec[b_][:, :, :], 0.0))
            link(g.memset(ident[:, :], 0.0))
            link(g.affine_select(out=ident[:, :], in_=ident[:, :], compare_op=ALU.not_equal, fill=1.0, base=0,
                                 pattern=[[-1, P]], channel_multiplier=1))
            g.affine_select(out=tri[:, :], in_=one[:, :], compare_op=ALU.is_gt, fill=0.0, base=0,
                            pattern=[[1, P]], channel_multiplier=-1).then_inc(s_const, 1)
            pool.wait_ge(s_const, 1)

            pool.wait_ge(s_dstl, 96)
            link(g.tensor_copy(dn_f[:, :], dn_i[:, :]))
            g.tensor_copy(ds_f[:, :], ds_i[:, :]).then_inc(s_dplane, 1)
            pool.wait_ge(s_dplane, 1)
            pool.wait_ge(s_cplane, 1)
            for q in range(COLS // PIECE):
                if q >= 2:
                    pool.wait_ge(s_ohu[1], q - 1)
                cols = slice(PIECE * q, PIECE * (q + 1))
                for oh, plane in ((hi_oh, hi_b), (lo_oh, lo_b)):
                    for k in range(HIST):
                        last = g.tensor_scalar(oh[q % 2][:, :, k], plane[:, cols], float(k), None, ALU.is_equal)
                last.then_inc(s_oh[1], 1)

            pool.wait_ge(s_idx, 1)

            def gather_attr(i, b_):
                pool.wait_ge(staged[b_], i + 1)
                pool.sem_inc(pool_blocks, 1)
                for t in range(BT):
                    g.indirect_dma_start(
                        out=attr[b_][:, t, :], out_offset=None, in_=edge_attr,
                        in_offset=bass.IndirectOffsetOnAxis(ap=stage_i[b_][:, t:t + 1], axis=0)).then_inc(gathered[b_], 16)

            def gather_x(i, b_):
                pool.wait_ge(staged2[b_], i + 1)
                pool.sem_inc(pool_blocks, 1)
                for t in range(BT):
                    g.indirect_dma_start(
                        out=xg[b_][:, t, :], out_offset=None, in_=T,
                        in_offset=bass.IndirectOffsetOnAxis(ap=stage_i[b_][:, t:t + 1], axis=0)).then_inc(gathered2[b_], 16)

            with g.Fori(0, LOOPS) as i:
                gather_attr(i, 0)
                gather_attr(i, 1)
            pool.wait_ge(s_fast, 1)
            with pool.If(pool.value_load(fast[0:1, 0:1], min_val=0, max_val=1)):
                pool.wait_ge(table_ok, 1)
                with g.Fori(0, LOOPS) as i:
                    gather_x(i, 0)
                    gather_x(i, 1)
            with pool.Else():
                def scatter(side, table):
                    with g.Fori(0, BLOCKS) as n:
                        pool.wait_ge(g_row_in[side], 16 * (n + 1))
                        pool.sem_inc(pool_blocks, 1)
                        pool.wait_ge(g_row_ok[side], n + 1)
                        pool.sem_inc(pool_blocks, 1)
                        for t in range(BT):
                            g.indirect_dma_start(
                                out=table, out_offset=bass.IndirectOffsetOnAxis(ap=stage_i[0][:, t:t + 1], axis=0),
                                in_=rec[0][:, t, 0:D], in_offset=None, compute_op=ALU.add).then_inc(g_sent[side], 16)
                    pool.wait_ge(g_sent[side], 16 * BT * BLOCKS)

                scatter(0, T)
                with g.Fori(0, BLOCKS) as n:
                    pool.wait_ge(g_edge, n + 1)
                    pool.sem_inc(pool_blocks, 1)
                    for t in range(BT):
                        g.indirect_dma_start(
                            out=source_i[:, t:t + 1], out_offset=None, in_=src.rearrange("(e a) -> e a", a=1),
                            in_offset=bass.IndirectOffsetOnAxis(ap=stage_i[0][:, t:t + 1], axis=0)).then_inc(g_source, 16)
                    pool.wait_ge(g_source, 16 * BT * (n + 1))
                    pool.sem_inc(pool_blocks, 1)
                    for t in range(BT):
                        g.indirect_dma_start(
                            out=xg[0][:, t, :], out_offset=None, in_=T,
                            in_offset=bass.IndirectOffsetOnAxis(ap=source_i[:, t:t + 1], axis=0)).then_inc(g_x, 16)
                scatter(1, out)

        @block.scalar
        def _(act):
            s = nc.scalar
            act.wait_ge(s_dturn, 1)
            for to, of in ((gi[1], p_z[0]), (rn[1], p_z[1])):
                last = s.copy(to[:, :].rearrange("c (n t) -> c t n", t=BT), of[:, :].rearrange("c (t n) -> c t n", n=P))
            last.then_inc(s_dcols, 1)
            act.wait_ge(s_wts, 1)
            act.wait_ge(s_idx, 1)

            def triple(i, b_):
                act.wait_ge(gathered[b_], 16 * BT * (i + 1))
                s.copy(attr3[b_][:, :, 0:2, :], attr[b_][:, :, :].unsqueeze(2).to_broadcast([P, BT, 2, FE]))
                for t in range(BT):
                    last = s.activation(attr3[b_][:, t, 2, :], attr[b_][:, t, :], ACT.Copy,
                                        scale=share[:, bass.ds(BT * (2 * i + b_) + t, 1)])
                last.then_inc(tripled[b_], 1)

            def hidden(i, b_):
                act.wait_ge(z_ok[b_], i + 1)
                s.activation(hid[b_][:, :], p_z[b_][:, :], ACT.Relu, bias=bias_z[:, :]).then_inc(hid_ok[b_], 1)

            def record(side, made, i, b_):
                act.wait_ge(made[b_], i + 1)
                if not isinstance(i, int) or i > 0:
                    act.wait_ge(rec_out[side][b_], 16 * i)
                s.copy(rec[b_][:, :, D], rn[side][:, bass.ds(BT * (2 * i + b_), BT)])
                s.copy(rec[b_][:, :, 0:D], p_m[b_][:, :, 0:D]).then_inc(rec_ok[side][b_], 1)

            def upper(side, j, b_):
                act.wait_ge(win_in[side][b_], 32 * (j + 1))
                if not isinstance(j, int) or j > 0:
                    act.wait_ge(exp_ok[side][b_], j)
                s.copy(upper_b[b_][:, :, :, :], win[b_][:, :, :, 0:D]).then_inc(hi_ok[side][b_], 1)

            def turn_src(i, b_, expand=True):
                if some(i, b_, -2):
                    triple(*back(i, b_, -2))
                if expand and some(i, b_, LAG - 1):
                    upper(0, *back(i, b_, LAG - 1))
                if some(i, b_, -1):
                    hidden(*back(i, b_, -1))
                if some(i, b_, 0):
                    record(0, m_ok, i, b_)

            triple(0, 0)
            triple(0, 1)
            hidden(0, 0)
            for n in range(LAG - 1):
                turn_src(n // 2, n % 2)

            def copy_x(i, b_):
                act.wait_ge(gathered2[b_], 16 * BT * (i + 1))
                if not isinstance(i, int) or i > 0:
                    act.wait_ge(h_ok[b_], i)
                s.copy(x1[b_][:, :, :], xg[b_][:, :, :]).then_inc(copied[b_], 1)

            def deviation(i, b_):
                act.wait_ge(var_ok[b_], i + 1)
                s.activation(sd[b_][:, :], mv[b_][:, :, 1], ACT.Sqrt, bias=eps_t[:, :]).then_inc(sd_ok[b_], 1)

            def normalize(i, b_):
                act.wait_ge(norm_ok[b_], i + 1)
                for t in range(BT):
                    last = s.activation(hn[b_][:, t, :], x1[b_][:, t, :], ACT.Relu,
                                        bias=nmr[b_][:, t:t + 1], scale=rstd[b_][:, t:t + 1])
                last.then_inc(h_ok[b_], 1)

            def take_turned(i, b_):
                act.wait_ge(ht_ok[b_], i + 1)
                s.copy(agg[b_][0:D, :], p_g[b_][0:D, :]).then_inc(hts_ok[b_], 1)

            act.wait_ge(s_fast, 1)
            with act.If(act.value_load(fast[0:1, 0:1], min_val=0, max_val=1)):
                turn_src(LAG // 2 - 1, 1)
                turns(s, turn_src, LAG // 2)

                def turn_dst(i, b_):
                    if some(i, b_, LAG):
                        upper(1, *back(i, b_, LAG))
                    if some(i, b_, 0):
                        deviation(i, b_)
                    if some(i, b_, -1):
                        copy_x(*back(i, b_, -1))
                    if some(i, b_, 0):
                        normalize(i, b_)
                    if some(i, b_, 1):
                        take_turned(*back(i, b_, 1))
                    if some(i, b_, 2):
                        record(1, y_ok, *back(i, b_, 2))

                for b_ in range(2):
                    act.wait_ge(rec_out[0][b_], 16 * LOOPS)
                copy_x(0, 0)
                turns(s, turn_dst, 0)
            with act.Else():
                turn_src(LAG // 2 - 1, 1, expand=False)
                turns(s, lambda i, b_: turn_src(i, b_, expand=False), LAG // 2)
                with s.Fori(0, BLOCKS) as n:
                    act.wait_ge(g_var, n + 1)
                    s.activation(sd[0][:, :], mv[0][:, :, 1], ACT.Sqrt, bias=eps_t[:, :]).then_inc(g_sd, 1)
                    act.wait_ge(g_norm, n + 1)
                    for t in range(BT):
                        last = s.activation(hn[0][:, t, :], xg[0][:, t, :], ACT.Relu,
                                            bias=nmr[0][:, t:t + 1], scale=rstd[0][:, t:t + 1])
                    last.then_inc(g_h, 1)

        @block.vector
        def _(dve):
            step = [0]
            v = nc.vector

            def link(ins):
                step[0] += 1
                ins.then_inc(s_v, 1)
                dve.wait_ge(s_v, step[0])

            v.memset(node_i[:, :], PAD).then_inc(s_pad, 1)
            dve.wait_ge(s_pool, 3)
            v.tensor_copy(pos_f[:, :], pos_i[:, :])
            v.tensor_scalar(low_i[:, :], pos_i[:, :], 2 ** LOW - 1, None, ALU.bitwise_and)
            link(v.tensor_scalar(srcs_i[:, :], pos_i[:, :], DUMMY - 1, None, ALU.bitwise_and))
            v.tensor_scalar(dummy_f[:, :], srcs_i[:, :], float(N), None, ALU.add)
            link(v.tensor_scalar(psign_i[:, :], psign_i[:, :], 1, None, ALU.bitwise_and))
            link(v.tensor_scalar(psign[:, :], psign_i[:, :], -2.0, 1.0, ALU.mult, ALU.add))
            for m in range(7):
                link(v.tensor_scalar(bit_a[:, :], prow_i[:, :], m, 1, ALU.logical_shift_right, ALU.bitwise_and))
                if m < 6:
                    link(v.tensor_scalar(bit_b[:, :], prow_i[:, :], m + 1, 1, ALU.logical_shift_right, ALU.bitwise_and))
                    link(v.tensor_tensor(bit_a[:, :], bit_a[:, :], bit_b[:, :], ALU.bitwise_xor))
                else:
                    link(v.tensor_copy(bit_b[:, :], bit_a[:, :]))
                    for q in range(BT):
                        v.tensor_copy(ha[:, q * P:(q + 1) * P], bit_b[:, :])
                link(v.tensor_scalar(flip[:, m, :], bit_a[:, :], -2.0, 1.0, ALU.mult, ALU.add))
            dve.wait_ge(s_w, 144)
            link(v.scalar_tensor_tensor(bias_z[:, :], w1u[:, :], u_s[:, 0:1], b1_s[:, :], ALU.mult, ALU.add))
            v.tensor_scalar(r0[:, :], bias_z[:, :].to_broadcast([P, P]), 0.0, None, ALU.max).then_inc(s_r0, 1)
            v.tensor_scalar(relub[:, :], b_bc[:, :], 0.0, None, ALU.max)
            dve.wait_ge(s_pw, 1)
            v.tensor_scalar(c_neg[:, :], p_t[:, 0:D], -1.0, None, ALU.mult)
            v.tensor_copy(wb_s[0:D, :], p_u[0:D, 0:D])
            link(v.tensor_tensor(c_bc[:, :], p_t[:, 0:D], b2_bc[:, :], ALU.add))

            def three_parts(row, to):
                link(v.tensor_copy(part_b[0][:, :], row[:, :]))
                link(v.tensor_tensor(part_f[0][:, :], row[:, :], part_b[0][:, :], ALU.subtract))
                link(v.tensor_copy(part_b[1][:, :], part_f[0][:, :]))
                link(v.tensor_tensor(part_f[1][:, :], part_f[0][:, :], part_b[1][:, :], ALU.subtract))
                link(v.tensor_scalar(part_f[1][:, :], part_f[1][:, :], ident[:, 2:3], None, ALU.mult))
                link(v.scalar_tensor_tensor(part_f[2][:, :], part_b[1][:, :], ident[:, 1:2], part_f[1][:, :], ALU.mult, ALU.add))
                link(v.scalar_tensor_tensor(part_f[1][:, :], part_b[0][:, :], ident[:, 0:1], part_f[2][:, :], ALU.mult, ALU.add))
                for q in range(to.shape[1]):
                    last = v.tensor_copy(to[:, q, :], part_f[1][:, :])
                link(last)

            dve.wait_ge(s_const, 1)
            three_parts(c_neg, nc3)
            three_parts(c_bc, c3[0])
            three_parts(b_bc, c3[1])
            v.tensor_copy(rowmax[:, :], eps_t[:, :]).then_inc(s_wts, 1)

            def count_planes(nodes):
                v.tensor_scalar(hi_i[:, :], nodes[:, :], 12, None, ALU.logical_shift_right)
                link(v.tensor_scalar(lo_i[:, :], nodes[:, :], 7, HIST - 1, ALU.logical_shift_right, ALU.bitwise_and))
                v.tensor_copy(hi_b[:, :], hi_i[:, :])
                v.tensor_copy(lo_b[:, :], lo_i[:, :]).then_inc(s_cplane, 1)

            def encode():
                v.tensor_scalar(tm[:, :], node_i[:, :], float(SPLIT), None, ALU.is_ge)
                link(v.tensor_scalar(td[:, :], node_i[:, :], 2.0, float(HIGH_ADD - LOW_TOP), ALU.mult, ALU.add))
                link(v.tensor_tensor(tm[:, :], tm[:, :], td[:, :], ALU.mult))
                link(v.tensor_scalar(td[:, :], node_i[:, :], -1.0, float(LOW_TOP), ALU.mult, ALU.add))
                link(v.tensor_tensor(kb[:, :].bitcast(I32), td[:, :], tm[:, :], ALU.add))
                link(v.tensor_scalar(kb[:, :].bitcast(I32), kb[:, :].bitcast(I32), LOW, None, ALU.logical_shift_left))
                link(v.tensor_tensor(ka[:, :].bitcast(I32), kb[:, :].bitcast(I32), low_i[:, :], ALU.bitwise_or))
                link(v.tensor_scalar(kb[:, :], ka[:, :], psign[:, :], None, ALU.mult))

            def pairs(tile, d):
                w = tile[:, :].rearrange("p (n t d) -> p n t d", t=2, d=d)
                return w[:, :, 0, :], w[:, :, 1, :]

            def mirror(tile, m):
                w = tile[:, :].rearrange("p (n m) -> p n m", m=m)
                return w[:, :, 0:m // 2], w[:, :, m // 2:m][:, :, ::-1]

            def sort(to_turn, turned_by):
                keys = [kb, ka]
                half = [ha, hb]

                def finish(ins, last):
                    if last:
                        ins.then_inc(to_turn, 1)
                    else:
                        link(ins)

                def exchange(view, arg, of=None, last=False):
                    lo, hi = view(keys[0] if of is None else of, arg)
                    to_lo, to_hi = view(keys[1], arg)
                    if of is not None:
                        link(v.tensor_copy(to_hi, hi))
                        hi = to_hi
                    v.tensor_tensor(to_lo, lo, hi, ALU.max)
                    finish(v.tensor_tensor(to_hi, lo, hi, ALU.min), last)
                    keys.reverse()

                def exchange_halves(d, of=None, half_of=None, last=False):
                    lo, hi = pairs(keys[0] if of is None else of, d)
                    to_lo, to_hi = pairs(keys[1], d)
                    hlo, hhi = pairs(half[0] if half_of is None else half_of, d)
                    to_hlo, to_hhi = pairs(half[1], d)
                    if of is not None:
                        v.tensor_copy(to_hi, hi)
                        link(v.tensor_copy(to_hhi, hhi))
                        hi, hhi = to_hi, to_hhi
                    first, _ = pairs(tm, d)
                    apart, _ = pairs(td, d)
                    v.tensor_tensor(first, lo, hi, ALU.is_ge)
                    link(v.tensor_tensor(apart, hlo, hhi, ALU.subtract))
                    v.tensor_tensor(to_lo, lo, hi, ALU.max)
                    v.tensor_tensor(to_hi, lo, hi, ALU.min)
                    link(v.tensor_tensor(first, first, apart, ALU.mult))
                    low_half = v.tensor_tensor(to_hlo, hhi, first, ALU.add)
                    if of is not None:
                        link(low_half)
                    finish(v.tensor_tensor(to_hhi, hlo, first, ALU.subtract), last)
                    keys.reverse()
                    half.reverse()

                for k in range(1, 10):
                    exchange(mirror, 2 ** k)
                    for q in range(k - 2, -1, -1):
                        exchange(pairs, 2 ** q, last=(k == 9 and q == 0))
                for k in range(10, 17):
                    assert keys[0] is key_tiles[turn_from[2 * (k - 10)]]
                    dve.wait_ge(turned_by, 2 * (k - 10) + 1)
                    link(v.tensor_tensor(keys[1][:, :].rearrange("c (b p) -> c b p", p=P),
                                         p_t[:, :].rearrange("c (b p) -> c b p", p=P),
                                         flip[:, k - 10:k - 9, :].to_broadcast([P, BT, P]), ALU.mult))
                    keys.reverse()
                    for q in range(k - 10, -1, -1):
                        if k < 16:
                            exchange(pairs, 2 ** q, last=q == 0)
                        else:
                            exchange_halves(2 ** q, last=q == 0)
                    assert keys[0] is key_tiles[turn_from[2 * (k - 10) + 1]]
                    dve.wait_ge(turned_by, 2 * (k - 10) + 2)
                    for q in range(8, -1, -1):
                        of = p_t if q == 8 else None
                        if k < 16:
                            exchange(pairs, 2 ** q, of=of, last=q == 0)
                        else:
                            exchange_halves(2 ** q, of=of, half_of=p_u if q == 8 else None)
                assert keys[0] is sorted_in and half[0] is ha

            def decode(ready):
                v.tensor_scalar(srcs_i[:, :], sorted_in[:, :].bitcast(I32), 2 ** LOW - 1, None, ALU.bitwise_and)
                link(v.tensor_scalar(node_i[:, :].bitcast(U32), sorted_in[:, :].bitcast(U32), LOW, None, ALU.logical_shift_right))
                v.tensor_scalar(tm[:, :], node_i[:, :], float(2 ** 16), None, ALU.is_ge)
                link(v.tensor_scalar(td[:, :], node_i[:, :], 2.0, -float(HIGH_ADD + LOW_TOP), ALU.mult, ALU.add))
                v.tensor_tensor(td[:, :], td[:, :], tm[:, :], ALU.mult)
                link(v.tensor_scalar(nodef[:, :], node_i[:, :], -1.0, float(LOW_TOP), ALU.mult, ALU.add))
                v.tensor_tensor(nodef[:, :], nodef[:, :], td[:, :], ALU.add).then_inc(s_line, 1)
                link(v.scalar_tensor_tensor(gidx_f[:, :], ha[:, :], float(HALF_E), srcs_i[:, :], ALU.mult, ALU.add))
                link(v.tensor_scalar(gidx_f[:, :], gidx_f[:, :], float(E - 1), None, ALU.min))

            turned_n = [14, 14]

            def to_columns(tile, turned_):
                return v.tensor_copy(tile[:, :].rearrange("c (n t) -> c t n", t=BT),
                                     turned_[:, :].rearrange("c (t n) -> c t n", n=P))

            def prepare(side, ka, kb):
                dve.wait_ge(s_nb, 32 * (side + 1))
                v.tensor_tensor(tm[:, :], nodef[:, :], prev_f[:, :], ALU.is_equal).then_inc(s_row, 1)
                dve.wait_ge(s_row, 1 + 3 * side)
                if side == 0:
                    link(v.tensor_scalar(td[:, :], tm[:, :], 2.0, -1.0, ALU.mult, ALU.add))
                    link(v.tensor_scalar(kb[:, :], tm[:, :], -1.0, 1.0, ALU.mult, ALU.add))
                    v.tensor_scalar(td[:, :], td[:, :], BIG, None, ALU.mult).then_inc(s_row, 1)
                    link(v.tensor_tensor(kb[:, :], kb[:, :], pos_f[:, :], ALU.mult))
                    v.reduce_max(rowmax[:, :], kb[:, :], AX.X).then_inc(s_tt[side], 1)
                    link(v.memset(pmax[:, 0:1], 0.0))
                    turned_n[side] += 1
                    dve.wait_ge(s_pt[side], turned_n[side])
                    link(v.tensor_copy(prev_f[0:1, 0:P], p_u[0:1, 0:P]))
                    v.tensor_tensor_scan(pmax[0:1, 1:P + 1], prev_f[0:1, 0:P], prev_f[0:1, 0:P], 0.0,
                                         ALU.max, ALU.max).then_inc(s_tt[side], 1)
                    turned_n[side] += 1
                    dve.wait_ge(s_pt[side], turned_n[side])
                    link(v.tensor_copy(carry_p[:, :], p_u[:, 256:257]))
                    link(v.tensor_tensor_scan(ka[:, :], kb[:, :], kb[:, :], carry_p[:, 0:1], ALU.max, ALU.max))
                    link(v.scalar_tensor_tensor(kb[:, :], ka[:, :], -1.0, pos_f[:, :], ALU.mult, ALU.add))
                    link(v.tensor_scalar(kb[:, :], kb[:, :], 1.0, None, ALU.add))
                    link(v.reciprocal(ha[:, :], kb[:, :]))
                    v.tensor_scalar(hb[:, :], ha[:, :], -1.0, 1.0, ALU.mult, ALU.add).then_inc(s_row, 1)
                    dve.wait_ge(s_row, 3)
                v.tensor_tensor(kb[:, :], nodef[:, :], next_f[:, :], ALU.not_equal)
                link(v.tensor_tensor(ka[:, :], nodef[:, :], dummy_f[:, :], ALU.subtract))
                v.tensor_tensor(ka[:, :], ka[:, :], kb[:, :], ALU.mult)
                link(v.scalar_tensor_tensor(kb[:, :], nodef[:, :], 1.0, kb[:, :], ALU.add, ALU.mult))
                v.tensor_scalar(kb[:, :], kb[:, :], -1.0, None, ALU.add)
                v.tensor_tensor(ka[:, :], ka[:, :], dummy_f[:, :], ALU.add).then_inc(s_tt[side], 1)
                turned_n[side] += 1
                dve.wait_ge(s_pt[side], turned_n[side])
                to_columns(gi[side], p_t)
                to_columns(sx, p_u).then_inc(s_tt[side], 1)
                turned_n[side] += 1
                dve.wait_ge(s_pt[side], turned_n[side])
                if side == 0:
                    to_columns(share, p_u)
                to_columns(rn[side], p_t).then_inc(s_idx, 1)

            def group_starts(side):
                c, d = cnt[:, :], HIST
                dve.wait_ge(s_ohu[side], COLS // PIECE)
                link(v.tensor_copy(c, p_h[0:d, 0, 0:d]))
                for q in range(1, BT):
                    link(v.tensor_tensor(c, p_h[d * q:d * (q + 1), 0, d * q:d * (q + 1)], c, ALU.add))
                v.tensor_tensor_scan(inc[:, :], c, zero[:, :], 0.0, ALU.add, ALU.add).then_inc(s_inc, 1)
                dve.wait_ge(s_base, 2 - side)
                link(v.tensor_copy(below[:, 0:1], p_h[0:d, 1, 0:1]))
                link(v.tensor_scalar(below[:, 1:d + 1], inc[:, :], below[:, 0:1], None, ALU.add))
                s0, s4 = below[:, 0:d:4], below[:, 4:d + 1:4]
                v.tensor_copy(first_i[side][:, :], s0).then_inc(s_first, 1)
                link(v.tensor_tensor(over[:, :], s4, s0, ALU.subtract))
                v.tensor_scalar(over[:, :], over[:, :], float(WROWS), None, ALU.is_gt)
                link(v.scalar_tensor_tensor(over2[:, :], s0, float(WROWS), limit[0:d, :], ALU.add, ALU.is_gt))
                link(v.tensor_tensor(over[:, :], over[:, :], over2[:, :], ALU.add))
                link(v.reduce_sum(wrong[0:25, side:side + 1], over[0:25, :], AX.X))

            dve.wait_ge(s_src, 64)
            encode()
            dve.wait_ge(s_dstl, 96)
            count_planes(dn_i)
            sort(s_tt[0], s_pt[0])
            decode(s_line)
            prepare(0, sorted_in, spare)

            def stage(n, b_, side, ok):
                v.tensor_copy(stage_i[b_][:, :], gi[side][:, bass.ds(BT * n, BT)]).then_inc(ok[b_], 1)

            dve.wait_ge(s_idx, 1)
            for b_ in range(2):
                stage(b_, b_, 0, staged)

            group_starts(1)
            link(v.tensor_copy(node_i[:, :], nodef[:, :]))
            count_planes(node_i)
            dve.wait_ge(s_cplane, 2)
            for q in range(COLS // PIECE):
                if q >= 2:
                    dve.wait_ge(s_ohu[0], q - 1)
                cols = slice(PIECE * q, PIECE * (q + 1))
                for oh, plane in ((hi_oh, hi_b), (lo_oh, lo_b)):
                    last = v.tensor_tensor(oh[q % 2][:, :, :], plane[:, cols].unsqueeze(2).to_broadcast([P, PIECE, HIST]),
                                           count_b[:, :].unsqueeze(1).to_broadcast([P, PIECE, HIST]), ALU.is_equal)
                last.then_inc(s_oh[0], 1)
            link(v.tensor_tensor(prev_f[:, 1:COLS], dn_f[:, 1:COLS], dn_f[:, 0:COLS - 1], ALU.is_lt))
            full = E // COLS
            v.reduce_sum(wrong[:, 2:3], prev_f[:, 1:COLS], AX.X)
            link(v.tensor_tensor(wrong[0:full, 3:4], pair[0:full, 1:2], pair[0:full, 0:1], ALU.is_lt))
            group_starts(0)
            v.reduce_sum(wrong1[:, :], wrong[:, :], AX.X).then_inc(s_wrong, 1)
            dve.wait_ge(s_wsum, 1)
            v.tensor_scalar(fast[:, :], p_h[0:1, 2, 0:1], 0.0, None, ALU.is_equal).then_inc(s_fast, 1)

            link(v.memset(carry[:, :], 0.0))

            def scans(i, b_):
                n = 2 * i + b_
                dve.wait_ge(turned[b_], i + 1)
                if some(i, b_, -2):
                    stage(n + 2, b_, 0, staged)
                dve.wait_ge(rows_in[b_], 16 * (i + 1))
                if not (isinstance(n, int) and n == 0):
                    dve.wait_ge(carried, n)
                f, c = feats[b_], c_rows[b_]
                v.tensor_tensor_scan(f[0:96, :], c[0:96, :], p_g[b_][0:96, :], carry[0:96, 0:1],
                                     ALU.mult, ALU.add).then_inc(summed, 1)
                dve.wait_ge(summed, n + 1)
                v.tensor_tensor_scan(f[32:64, :], c[96:128, :], p_g[b_][32:64, :], carry[32:64, 0:1],
                                     ALU.min, ALU.max).then_inc(feats_ok[b_], 1)
                dve.wait_ge(feats_ok[b_], i + 1)
                v.tensor_copy(carry[:, :], f[:, BLK - 1:BLK]).then_inc(carried, 1)

            def onehots(side, j, b_):
                m = 2 * j + b_
                dve.wait_ge(win_in[side][b_], 32 * (j + 1))
                v.tensor_tensor(rel[b_][:, :, :], win[b_][:, :, :, D],
                                base_f[:, bass.ds(2 * m, 2)].unsqueeze(2).to_broadcast([P, 2, 3]),
                                ALU.subtract).then_inc(rel_ok[side][b_], 1)
                if not isinstance(j, int) or j > 0:
                    dve.wait_ge(exp_ok[side][b_], j)
                dve.wait_ge(rel_ok[side][b_], j + 1)
                for g in range(2):
                    for a in range(3):
                        lo, w = (512 * a, 512) if a < 2 else (1024, 256)
                        v.tensor_scalar(oneh[b_][:, g, lo:lo + w], node_of[:, GROUP - w:GROUP],
                                        rel[b_][:, g, a:a + 1], None, ALU.is_equal)
                dve.wait_ge(hi_ok[side][b_], j + 1)
                v.tensor_tensor(rest[b_][:, :, :, :], win[b_][:, :, :, 0:D], upper_b[b_][:, :, :, :],
                                ALU.subtract).then_inc(rest_ok[side][b_], 1)
                dve.wait_ge(rest_ok[side][b_], j + 1)
                v.tensor_tensor(lower_b[b_][:, :, :, :], rest[b_][:, :, :, :], middle_of(b_), ALU.subtract).then_inc(lo_ok[side][b_], 1)

            def add_dense(side, j, b_):
                end = isinstance(j, int) and 2 * j + b_ == BLOCKS - 1 and side == 0
                dve.wait_ge(exp_ok[side][b_], j + 1)
                dve.wait_ge(d_in[side][b_], 16 * (j + 1) + (16 if end else 0))
                if not isinstance(j, int) or j > 0:
                    dve.wait_ge(d_out[side][b_], 16 * j)
                if side == 0:
                    ins = v.tensor_tensor(dout[b_][:, :], p_e[b_][:, :], din[b_][:, :], ALU.add)
                else:
                    ins = v.scalar_tensor_tensor(dout[b_][:, :], p_e[b_][:, :], 0.0, din[b_][:, :], ALU.max, ALU.add)
                ins.then_inc(sum_ok[side][b_], 1)

            def turn_src(i, b_, expand=True):
                if some(i, b_, 0):
                    scans(i, b_)
                if expand and some(i, b_, LAG):
                    onehots(0, *back(i, b_, LAG))
                if expand and some(i, b_, LAG + 2):
                    add_dense(0, *back(i, b_, LAG + 2))

            for n in range(LAG):
                turn_src(n // 2, n % 2)
            dve.wait_ge(s_fast, 1)
            links = step[0]
            with dve.If(dve.value_load(fast[0:1, 0:1], min_val=0, max_val=1)):
                turns(v, turn_src, LAG // 2)
                dve.wait_ge(s_dcols, 1)
                for b_ in range(2):
                    stage(b_, b_, 1, staged2)

                def moments(i, b_):
                    dve.wait_ge(copied[b_], i + 1)
                    if some(i, b_, -2):
                        stage(2 * i + 2 + b_, b_, 1, staged2)
                    for t in range(BT):
                        last = v.bn_stats(stat[b_][:, t, :], x1[b_][:, t, :])
                    last.then_inc(stat_ok[b_], 1)
                    dve.wait_ge(stat_ok[b_], i + 1)
                    v.tensor_copy(rowmax[:, :], eps_t[:, :])
                    for t in range(BT):
                        last = v.bn_aggr(mv[b_][:, t, :], stat[b_][:, t, :])
                    last.then_inc(var_ok[b_], 1)

                def norm(i, b_):
                    dve.wait_ge(sd_ok[b_], i + 1)
                    v.reciprocal(rstd[b_][:, :], sd[b_][:, :]).then_inc(rstd_ok[b_], 1)
                    dve.wait_ge(rstd_ok[b_], i + 1)
                    v.scalar_tensor_tensor(nmr[b_][:, :], mv[b_][:, :, 0], -1.0, rstd[b_][:, :],
                                           ALU.mult, ALU.mult).then_inc(norm_ok[b_], 1)

                def turn_dst(i, b_):
                    if some(i, b_, 0):
                        moments(i, b_)
                    if some(i, b_, LAG):
                        onehots(1, *back(i, b_, LAG))
                    if some(i, b_, 0):
                        norm(i, b_)
                    if some(i, b_, LAG + 2):
                        add_dense(1, *back(i, b_, LAG + 2))

                turns(v, turn_dst, 0)
            with dve.Else():
                step[0] = links
                turns(v, lambda i, b_: turn_src(i, b_, expand=False), LAG // 2)

                def dense(side, row):
                    def step(n, parts=1):
                        dve.wait_ge(g_dense_in[side], 16 * (n + parts))
                        v.tensor_tensor(dout[0][:, :].rearrange("p (q d) -> p q d", d=D),
                                        din[0][:, :].rearrange("p (q d) -> p q d", d=D),
                                        row[:, :].unsqueeze(1).to_broadcast([P, 2 * BT, D]), ALU.add).then_inc(g_dense_ok[side], 1)
                        dve.wait_ge(g_dense_out[side], 16 * (n + 1))
                        v.tensor_copy(rowmax[:, :], eps_t[:, :])

                    with v.Fori(0, BLOCKS - 1) as n:
                        step(n)
                    step(BLOCKS - 1, parts=2 if side == 0 else 1)

                def stage_targets(side):
                    with v.Fori(0, BLOCKS) as n:
                        v.tensor_copy(stage_i[0][:, :], sx[:, bass.ds(BT * n, BT)]).then_inc(g_row_ok[side], 1)
                        dve.wait_ge(g_sent[side], 16 * BT * (n + 1))
                        v.tensor_copy(rowmax[:, :], eps_t[:, :])

                dense(0, c_bc)
                stage_targets(0)
                v.memset(node_i[:, :], PAD).then_inc(g_pad, 1)
                for q in range(BT):
                    v.tensor_copy(ha[:, q * P:(q + 1) * P], bit_b[:, :])
                dve.wait_ge(g_dst_in, 64)
                encode()
                sort(s_tt[1], s_pt[1])
                decode(s_line)
                prepare(1, sorted_in, spare)
                dve.wait_ge(g_rows_stored, 16)
                dense(1, relub)
                link(v.memset(carry[:, :], 0.0))
                with v.Fori(0, BLOCKS) as n:
                    v.tensor_copy(stage_i[0][:, :], gi[1][:, bass.ds(BT * n, BT)]).then_inc(g_edge, 1)
                    dve.wait_ge(g_x, 16 * BT * (n + 1))
                    for t in range(BT):
                        last = v.bn_stats(stat[0][:, t, :], xg[0][:, t, :])
                    last.then_inc(g_stat, 1)
                    dve.wait_ge(g_stat, n + 1)
                    v.tensor_copy(rowmax[:, :], eps_t[:, :])
                    for t in range(BT):
                        last = v.bn_aggr(mv[0][:, t, :], stat[0][:, t, :])
                    last.then_inc(g_var, 1)
                    dve.wait_ge(g_sd, n + 1)
                    v.reciprocal(rstd[0][:, :], sd[0][:, :]).then_inc(g_rstd, 1)
                    dve.wait_ge(g_rstd, n + 1)
                    v.scalar_tensor_tensor(nmr[0][:, :], mv[0][:, :, 0], -1.0, rstd[0][:, :], ALU.mult, ALU.mult).then_inc(g_norm, 1)
                    dve.wait_ge(g_ht, n + 1)
                    v.tensor_copy(rowmax[:, :], eps_t[:, :])
                    dve.wait_ge(g_c, 16 * (n + 1))
                    v.tensor_tensor_scan(agg[0][0:D, :], c_rows[0][0:D, :], p_g[0][0:D, :], carry[0:D, 0:1],
                                         ALU.mult, ALU.add).then_inc(g_agg, 1)
                    dve.wait_ge(g_agg, n + 1)
                    v.tensor_copy(carry[0:D, :], agg[0][0:D, BLK - 1:BLK]).then_inc(g_carry, 1)
                    dve.wait_ge(g_y, n + 1)
                    v.scalar_tensor_tensor(rec[0][:, :, 0:D], p_m[0][:, :, 0:D], 0.0,
                                           relub[:, :].unsqueeze(1).to_broadcast([P, BT, D]),
                                           ALU.max, ALU.subtract).then_inc(g_rec, 1)
                    dve.wait_ge(g_stored, 16 * (n + 1))
                    v.tensor_copy(rowmax[:, :], eps_t[:, :])
                    dve.wait_ge(g_carry, n + 1)
                    v.tensor_copy(carry_p[:, :], eps_t[:, :])
                stage_targets(1)

        @block.tensor
        def _(pe):
            mm = nc.tensor.matmul
            tr = nc.tensor.transpose
            pe.wait_ge(s_const, 1)
            pe.wait_ge(s_r0, 1)
            mm(p_t[:, 0:D], r0[:, :], w2_s[:, :], start=True, stop=True)
            tr(p_u[0:D, 0:D], w_s[:, :], ident[0:D, 0:D]).then_inc(s_pw, 1)
            pe.wait_ge(s_wts, 1)

            def turn(to, of):
                for q in range(BT):
                    last = tr(to[:, q * P:(q + 1) * P], of[:, q * P:(q + 1) * P], ident[:, :])
                return last

            def turn_columns(to, of):
                for t in range(BT):
                    last = tr(to[:, t * P:(t + 1) * P], of[:, t::BT], ident[:, :])
                return last

            def count(side, q):
                pe.wait_ge(s_oh[side], q + 1)
                for c in range(0, PIECE, BT):
                    last = mm(p_h[:, 0, :], hi_oh[q % 2][:, c:c + BT, :].rearrange("p c k -> p (c k)"),
                              lo_oh[q % 2][:, c:c + BT, :].rearrange("p c k -> p (c k)"),
                              start=(q == 0 and c == 0), stop=(q == COLS // PIECE - 1 and c == PIECE - BT))
                last.then_inc(s_ohu[side], 1)

            def count_base(side):
                pe.wait_ge(s_inc, 2 - side)
                mm(p_h[0:HIST, 1, 0:1], tri[0:HIST, 0:HIST], inc[:, HIST - 1:HIST], start=True, stop=True).then_inc(s_base, 1)

            def sort_turns(to_turn, turned_by, between):
                for t, which in enumerate(turn_from):
                    pe.wait_ge(to_turn, t + 1)
                    last = turn(p_t, key_tiles[which])
                    if t == 13:
                        last = turn(p_u, hb)
                    last.then_inc(turned_by, 1)
                    between(t)

            pe.wait_ge(s_dplane, 1)
            turn_columns(p_z[0], ds_f)
            turn_columns(p_z[1], dn_f).then_inc(s_dturn, 1)
            count(1, 0)
            count(1, 1)
            sort_turns(s_tt[0], s_pt[0], lambda t: count(1, t // 2 + 2) if t % 2 and t < 12 else None)
            pe.wait_ge(s_tt[0], 15)
            tr(p_u[0:1, 0:P], rowmax[:, :], ident[:, :]).then_inc(s_pt[0], 1)
            pe.wait_ge(s_tt[0], 16)
            mm(p_u[:, 256:257], pmax[0:1, 0:P], one[0:1, 0:1], start=True, stop=True).then_inc(s_pt[0], 1)
            pe.wait_ge(s_tt[0], 17)
            turn_columns(p_t, gidx_f)
            turn_columns(p_u, sorted_in).then_inc(s_pt[0], 1)
            pe.wait_ge(s_tt[0], 18)
            turn_columns(p_t, spare)
            turn_columns(p_u, ha).then_inc(s_pt[0], 1)
            count_base(1)
            for q in range(COLS // PIECE):
                count(0, q)
            count_base(0)
            pe.wait_ge(s_wrong, 1)
            mm(p_h[0:1, 2, 0:1], wrong1[:, 0:1], one[:, 0:1], start=True, stop=True).then_inc(s_wsum, 1)
            pe.wait_ge(s_fast, 1)
            pe.wait_ge(s_dcols, 1)

            def turn_attr(i, b_):
                pe.wait_ge(tripled[b_], i + 1)
                for t in range(BT):
                    last = tr(p_g[b_][0:96, t::BT],
                              attr3[b_][:, t, :, :].rearrange("p a f -> p (a f)"), ident[:, :])
                last.then_inc(turned[b_], 1)

            def layer1(i, b_):
                pe.wait_ge(feats_ok[b_], i + 1)
                mm(p_z[b_][:, :], w1_s[:, :], feats[b_][:, :], start=True, stop=True).then_inc(z_ok[b_], 1)

            def layer2(i, b_):
                pe.wait_ge(hid_ok[b_], i + 1)
                mm(p_m[b_][:, :, 0:D], one_b[0:3, :], nc3[0:3, :, :], start=True, stop=False)
                for t in range(BT):
                    last = mm(p_m[b_][:, t, 0:D], hid[b_][:, t::BT], w2_s[:, :], start=False, stop=t == BT - 1)
                last.then_inc(m_ok[b_], 1)

            def expand(side, j, b_):
                pe.wait_ge(lo_ok[side][b_], j + 1)
                if not isinstance(j, int) or j > 0:
                    pe.wait_ge(sum_ok[side][b_], j)
                mm(p_e[b_][:, :], one_b[0:3, :], c3[side][0:3, :, :].rearrange("p q d -> p (q d)"), start=True, stop=False)
                parts = (upper_b[b_][:, :, :, :], middle_of(b_), lower_b[b_][:, :, :, :])
                for g in range(2):
                    for h in range(2):
                        for t in range(2):
                            q = (2 * g + h) * 2 + t
                            for a in range(2 + h):
                                at = 512 * a + (256 * h if a < 2 else 0) + P * t
                                for w in range(3):
                                    last = mm(p_e[b_][:, q * D:(q + 1) * D], oneh[b_][:, g, at:at + P],
                                              parts[w][:, g, a, :], start=False, stop=(q == 7 and a == 2 and w == 2))
                last.then_inc(exp_ok[side][b_], 1)

            turn_attr(0, 0)
            turn_attr(0, 1)
            layer1(0, 0)

            def turn_src(i, b_, expand_=True):
                if some(i, b_, -2):
                    turn_attr(*back(i, b_, -2))
                if some(i, b_, -1):
                    layer1(*back(i, b_, -1))
                if some(i, b_, 0):
                    layer2(i, b_)
                if expand_ and some(i, b_, LAG):
                    expand(0, *back(i, b_, LAG))

            for n in range(LAG - 1):
                turn_src(n // 2, n % 2)
            with pe.If(pe.value_load(fast[0:1, 0:1], min_val=0, max_val=1)):
                turn_src(LAG // 2 - 1, 1)
                turns(nc.tensor, turn_src, LAG // 2)

                def turn_h(i, b_):
                    pe.wait_ge(h_ok[b_], i + 1)
                    pe.sem_inc(pe_blocks, 1)
                    for t in range(BT):
                        last = tr(p_g[b_][0:D, t * P:(t + 1) * P], hn[b_][:, t, :], ident[:, :])
                    last.then_inc(ht_ok[b_], 1)

                def conv(i, b_):
                    pe.wait_ge(hts_ok[b_], i + 1)
                    for t in range(BT):
                        last = mm(p_m[b_][:, t, 0:D], agg[b_][0:D, t * P:(t + 1) * P], wb_s[0:D, :], start=True, stop=True)
                    last.then_inc(y_ok[b_], 1)

                def turn_dst(i, b_):
                    if some(i, b_, LAG + 1):
                        expand(1, *back(i, b_, LAG + 1))
                    if some(i, b_, 0):
                        turn_h(i, b_)
                    if some(i, b_, 2):
                        conv(*back(i, b_, 2))

                turns(nc.tensor, turn_dst, 0)
            with pe.Else():
                turn_src(LAG // 2 - 1, 1, expand_=False)
                turns(nc.tensor, lambda i, b_: turn_src(i, b_, expand_=False), LAG // 2)
                sort_turns(s_tt[1], s_pt[1], lambda t: None)
                pe.wait_ge(s_tt[1], 15)
                turn_columns(p_t, gidx_f)
                turn_columns(p_u, sorted_in).then_inc(s_pt[1], 1)
                pe.wait_ge(s_tt[1], 16)
                turn_columns(p_t, spare).then_inc(s_pt[1], 1)
                with nc.tensor.Fori(0, BLOCKS) as n:
                    pe.wait_ge(g_h, n + 1)
                    pe.sem_inc(pe_blocks, 1)
                    for t in range(BT):
                        last = tr(p_g[0][0:D, t::BT], hn[0][:, t, :], ident[:, :])
                    last.then_inc(g_ht, 1)
                    pe.wait_ge(g_agg, n + 1)
                    for t in range(BT):
                        last = mm(p_m[0][:, t, 0:D], agg[0][0:D + 1, t::BT], wb_s[:, :], start=True, stop=True)
                    last.then_inc(g_y, 1)


_INS = ['x', 'src', 'dst', 'edge_attr_32', 'L0_gnn_u', 'L0_gnn_W1', 'L0_gnn_b1', 'L0_gnn_W2', 'L0_gnn_b2',
        'L1_gnn_W', 'L1_gnn_b']


def kernel(**inputs):
    import numpy as _np
    import concourse.bacc as _bacc
    from concourse import mybir as _mybir
    from concourse.bass_utils import run_bass_kernel_spmd as _run

    nc = _bacc.Bacc("TRN2", target_bir_lowering=False, num_devices=1)
    arrays, args = {}, []
    for name in _INS:
        a = _np.ascontiguousarray(inputs[name])
        arrays[f"in_{name}_dram"] = a
        args.append(nc.dram_tensor(f"in_{name}_dram", a.shape, _mybir.dt.from_np(a.dtype), kind="ExternalInput").ap())
    args.append(nc.dram_tensor("out_dram", (ROWS, D), _mybir.dt.float32, kind="ExternalOutput").ap())
    build(nc, *args)
    r = _run(nc, [arrays], core_ids=[0])
    return r.results[0]["out_dram"][:N]
```

```python
from contextlib import ExitStack

import concourse.bass as bass
from concourse import mybir

F32 = mybir.dt.float32
I32 = mybir.dt.int32
U32 = mybir.dt.uint32
BF16 = mybir.dt.bfloat16
F16 = mybir.dt.float16
ALU = mybir.AluOpType
ACT = mybir.ActivationFunctionType
AX = mybir.AxisListType

P = 128
N = 100000
E = 50000
FE = 32
D = 64
HID = 128
EPS = 1e-5

COLS = 512
POS = P * COLS
BT = 4
BLK = BT * P
BLOCKS = -(-E // BLK)
LOOPS = BLOCKS // 2
SRC_LAG = 6
DST_LAG = 8
GROUP = 512
STEP = 2 * GROUP
WROWS = 3 * P
REC = 66
WIDE = 1280
GROUPS = 200
SPAN = 5
PAD = GROUPS * GROUP
DUMMY = 2 * BLK
ROWS = N + DUMMY
SPARE = ROWS - BLOCKS * STEP
HALF_E = E // 2
LOW = 15
SPLIT = 507 * P
LOW_TOP = SPLIT + 255
HIGH_ADD = 2 ** 16 + 256 - SPLIT
BIG = 3.4028e38
assert SPARE % 96 == 0 and SPARE // 96 * D >= BT * REC and BLOCKS % 2 == 0 and N <= BLOCKS * STEP <= ROWS
assert HALF_E < 2 ** LOW and LOW_TOP < 255 * 256 and PAD + HIGH_ADD < 2 ** 17


def back(i, b_, k):
    return i + (b_ - k) // 2, (b_ - k) % 2


def some(i, b_, k):
    return not isinstance(i, int) or 0 <= 2 * i + b_ - k < BLOCKS


def turns(eng, turn, start, lag):
    inner = lag // 2 + 2
    for i in range(start, inner):
        turn(i, 0)
        turn(i, 1)
    with eng.Fori(inner, LOOPS - 1) as i:
        turn(i, 0)
        turn(i, 1)
    for i in range(LOOPS - 1, LOOPS + lag // 2 + 2):
        turn(i, 0)
        turn(i, 1)


def build(nc, x, src, dst, edge_attr, u, W1, b1, W2, b2, W, b, out):
    T = nc.dram_tensor("node_table", [ROWS, D], F32).ap()
    line = nc.dram_tensor("node_line", [2, POS + 2], F32).ap()
    rows_src = nc.dram_tensor("rows_src", [4, POS], F32).ap()
    rows_dst = nc.dram_tensor("rows_dst", [1, POS], F32).ap()
    recs = [nc.dram_tensor(f"records{s}", [(BLOCKS + 1) * BLK, REC], F32).ap() for s in range(2)]

    with ExitStack() as ctx:
        def sb(name, shape, dt=F32):
            return ctx.enter_context(nc.sbuf_tensor(name, shape, dt))

        def ps(name, shape):
            return ctx.enter_context(nc.psum_tensor(name, shape, F32))

        def sem(name):
            return ctx.enter_context(nc.semaphore(name))

        def two(name):
            return [sem(f"{name}_{b_}") for b_ in range(2)]

        ident = sb("ident", [P, P])
        one = sb("one", [P, P])
        one_b = sb("one_b", [P, P], BF16)
        pos_i = sb("pos_i", [P, COLS], I32)
        pos_f = sb("pos_f", [P, COLS])
        low_i = sb("low_i", [P, COLS], I32)
        dummy_f = sb("dummy_f", [P, COLS])
        prow_i = sb("prow_i", [P, P], I32)
        bit_a = sb("bit_a", [P, P], I32)
        bit_b = sb("bit_b", [P, P], I32)
        flip = sb("flip", [P, 7, P])
        psign_i = sb("psign_i", [P, 1], I32)
        psign = sb("psign", [P, 1])
        eps_t = sb("eps_t", [P, 1])
        guard = sb("guard", [1, 2])
        node_i16 = sb("node_i16", [P, GROUP], I32)
        node_of = sb("node_of", [P, GROUP], F16)
        base_i = sb("base_i", [P, GROUPS], I32)
        base_f = sb("base_f", [P, GROUPS])
        span_f = sb("span_f", [P, SPAN])
        limit_i = sb("limit_i", [P, GROUPS], I32)
        limit = sb("limit", [P, GROUPS])
        pad_rec = sb("pad_rec", [P, SPARE // 96 * D])
        w1_s = sb("w1_s", [96, HID])
        w1u = sb("w1u", [P, 1])
        b1_s = sb("b1_s", [P, 1])
        u_s = sb("u_s", [P, 1])
        w2_s = sb("w2_s", [P, D])
        b2_bc = sb("b2_bc", [P, D])
        w_s = sb("w_s", [D, D])
        b_bc = sb("b_bc", [P, D])
        wb_s = sb("wb_s", [D + 1, D])
        bias_z = sb("bias_z", [P, 1])
        r0 = sb("r0", [P, P])
        c_neg = sb("c_neg", [P, D])
        c3 = [sb(f"c3_{s}", [P, 2 * BT, D], BF16) for s in range(2)]
        nc3 = sb("nc3", [P, BT, D], BF16)
        part_b = [sb(f"part_b{q}", [P, D], BF16) for q in range(2)]
        part_f = [sb(f"part_f{q}", [P, D]) for q in range(3)]
        c_bc = sb("c_bc", [P, D])
        relub = sb("relub", [P, D])
        node_i = sb("node_i", [P, COLS], I32)
        srcs_i = sb("srcs_i", [P, COLS], I32)
        ka = sb("ka", [P, COLS])
        kb = sb("kb", [P, COLS])
        ha = sb("ha", [P, COLS])
        hb = sb("hb", [P, COLS])
        tm = sb("tm", [P, COLS])
        td = sb("td", [P, COLS])
        nodef = sb("nodef", [P, COLS])
        gidx_f = sb("gidx_f", [P, COLS])
        prev_f = sb("prev_f", [P, COLS])
        next_f = sb("next_f", [P, COLS])
        rowmax = sb("rowmax", [P, 1])
        pmax = sb("pmax", [1, P + 1])
        carry_p = sb("carry_p", [P, 1])
        dn_i = sb("dn_i", [P, COLS], I32)
        ds_i = sb("ds_i", [P, COLS], I32)
        dn_f = sb("dn_f", [P, COLS])
        ds_f = sb("ds_f", [P, COLS])
        pair = sb("pair", [P, 2], I32)
        gi = [sb(f"gi{s}", [P, COLS], I32) for s in range(2)]
        share = sb("share", [P, COLS])
        sx = sb("sx", [P, COLS], I32)
        rn = [sb(f"rn{s}", [P, COLS]) for s in range(2)]
        low_node_i = sb("low_node_i", [P, 2], I32)
        low_node = sb("low_node", [P, 1])
        bound = sb("bound", [P, SPAN])
        signs = sb("signs", [P, SPAN])
        less = sb("less", [P, SPAN + 1])
        in_group = sb("in_group", [P, SPAN])
        above = sb("above", [P, SPAN, GROUPS])
        sign_out = sb("sign_out", [P, COLS])
        over = sb("over", [1, GROUPS])
        over2 = sb("over2", [1, GROUPS])
        start_row = [sb(f"start_row{s}", [1, GROUPS], I32) for s in range(2)]
        start_f = sb("start_f", [1, GROUPS])
        wrong = sb("wrong", [P, 6])
        wrong1 = sb("wrong1", [P, 1])
        fast = sb("fast", [1, 1], I32)
        stage_i = [sb(f"stage_i{b_}", [P, BT], I32) for b_ in range(2)]
        source_i = sb("source_i", [P, BT], I32)
        attr = [sb(f"attr{b_}", [P, BT, FE]) for b_ in range(2)]
        attr3 = [sb(f"attr3_{b_}", [P, BT, 3, FE]) for b_ in range(2)]
        c_rows = [sb(f"c_rows{b_}", [P, BLK]) for b_ in range(2)]
        feats = [sb(f"feats{b_}", [96, BLK]) for b_ in range(2)]
        carry = sb("carry", [96, 1])
        hid = [sb(f"hid{b_}", [P, BLK]) for b_ in range(2)]
        rec = [sb(f"rec{b_}", [P, BT, REC]) for b_ in range(2)]
        win = [sb(f"win{b_}", [P, 2, 3, REC]) for b_ in range(2)]
        rel = [sb(f"rel{b_}", [P, 2, 3]) for b_ in range(2)]
        oneh = [sb(f"oneh{b_}", [P, 2, WIDE], BF16) for b_ in range(2)]
        upper_b = [sb(f"upper_b{b_}", [P, 2, 3, D], BF16) for b_ in range(2)]
        rest = [sb(f"rest{b_}", [P, 2, 3, D]) for b_ in range(2)]
        lower_b = [sb(f"lower_b{b_}", [P, 2, 3, D], BF16) for b_ in range(2)]
        din = [sb(f"din{b_}", [P, 2 * BT * D]) for b_ in range(2)]
        dout = [sb(f"dout{b_}", [P, 2 * BT * D]) for b_ in range(2)]
        xg = [sb(f"xg{b_}", [P, BT, D]) for b_ in range(2)]
        x1 = [sb(f"x1_{b_}", [P, BT, D]) for b_ in range(2)]
        stat = [sb(f"stat{b_}", [P, BT, 6]) for b_ in range(2)]
        mv = [sb(f"mv{b_}", [P, BT, 2]) for b_ in range(2)]
        sd = [sb(f"sd{b_}", [P, BT]) for b_ in range(2)]
        rstd = [sb(f"rstd{b_}", [P, BT]) for b_ in range(2)]
        nmr = [sb(f"nmr{b_}", [P, BT]) for b_ in range(2)]
        hn = [sb(f"hn{b_}", [P, BT, D]) for b_ in range(2)]
        agg = [sb(f"agg{b_}", [D + 1, BLK]) for b_ in range(2)]

        p_g = [ps(f"p_g{b_}", [P, BLK]) for b_ in range(2)]
        p_z = [ps(f"p_z{b_}", [P, BLK]) for b_ in range(2)]
        p_m = [ps(f"p_m{b_}", [P, BT, P]) for b_ in range(2)]
        p_t = ps("p_t", [P, COLS])
        p_u = ps("p_u", [P, COLS])
        p_e = [p_t, p_u]
        p_s = p_m[1][:, :, :].rearrange("p t c -> p (t c)")

        s_w = sem("weights_loaded")
        s_const = sem("constants_made")
        s_pool = sem("pool_step")
        s_v = sem("vector_step")
        s_src = sem("src_loaded")
        s_pad = sem("pads_set")
        s_dpad = sem("dst_pads_set")
        s_dstl = sem("dst_loaded")
        s_dplane = sem("dst_planes")
        s_dturn = sem("dst_turned")
        s_dcols = sem("dst_columns")
        s_bound = sem("bounds_made")
        s_signs = sem("signs_summed")
        s_above = sem("above_made")
        s_base = sem("starts_summed")
        s_wrong = sem("wrong_counted")
        s_wsum = sem("wrong_summed")
        s_fast = sem("choice_made")
        table_ok = sem("table_ok")
        s_tail = sem("tail_filled")
        s_tt = two("to_turn")
        s_pt = two("pe_turned")
        s_pw = sem("pe_weights")
        s_line = sem("line_ready")
        s_lw = sem("line_written")
        s_nb = sem("neighbours_loaded")
        s_row = sem("rows_ready")
        s_rw = sem("rows_written")
        s_idx = sem("indices_ready")
        s_wts = sem("weights_ready")
        pool_blocks = sem("pool_blocks")
        pe_blocks = sem("pe_blocks")
        sp_steps = sem("sp_steps")
        s_r0 = sem("r0_ready")

        staged, gathered, rows_in = two("staged"), two("gathered"), two("rows_in")
        tripled, turned, feats_ok = two("tripled"), two("turned"), two("feats_ok")
        z_ok, hid_ok, m_ok = two("z_ok"), two("hid_ok"), two("m_ok")
        carried, summed = sem("carried"), sem("summed")
        rec_ok = [two(f"rec_ok{s}") for s in range(2)]
        rec_out = [two(f"rec_out{s}") for s in range(2)]
        win_in = [two(f"win_in{s}") for s in range(2)]
        d_in = [two(f"dense_in{s}") for s in range(2)]
        rel_ok = [two(f"rel_ok{s}") for s in range(2)]
        hi_ok = [two(f"upper_part_ok{s}") for s in range(2)]
        rest_ok = [two(f"rest_ok{s}") for s in range(2)]
        lo_ok = [two(f"lower_part_ok{s}") for s in range(2)]
        exp_ok = [two(f"expanded{s}") for s in range(2)]
        sum_ok = [two(f"added{s}") for s in range(2)]
        d_out = [two(f"dense_out{s}") for s in range(2)]
        staged2, gathered2, copied = two("staged2"), two("gathered2"), two("copied")
        stat_ok, var_ok, sd_ok = two("stat_ok"), two("var_ok"), two("sd_ok")
        rstd_ok, norm_ok, h_ok, ht_ok = two("rstd_ok"), two("norm_ok"), two("h_ok"), two("ht_ok")
        hts_ok, y_ok = two("hts_ok"), two("y_ok")

        g_dense_in, g_dense_ok, g_dense_out = d_in[0], sum_ok[0], d_out[0]
        g_row_in, g_row_ok, g_sent = win_in[0], rel_ok[0], exp_ok[0]
        g_pad, g_dst_in, g_rows_stored = rel_ok[1][0], win_in[1][0], win_in[1][1]
        g_edge, g_source, g_x = staged2[0], gathered2[0], gathered2[1]
        g_stat, g_var, g_sd = stat_ok[0], var_ok[0], sd_ok[0]
        g_rstd, g_norm, g_h, g_ht = rstd_ok[0], norm_ok[0], h_ok[0], ht_ok[0]
        g_c, g_agg, g_carry = d_in[1][0], hts_ok[0], hts_ok[1]
        g_y, g_rec, g_stored = y_ok[0], rec_ok[1][0], rec_out[1][0]

        turn_from, moves = [], 9 * 10 // 2
        for k in range(10, 17):
            turn_from.append(moves % 2)
            moves += 1 + (k - 9)
            turn_from.append(moves % 2)
            moves += 9
        key_tiles = [kb, ka]
        sorted_in, spare = key_tiles[moves % 2], key_tiles[1 - moves % 2]
        block = ctx.enter_context(nc.Block())

        def as_row(c):
            return c.rearrange("(a n) -> a n", a=1)

        def as_rows(c):
            return c.rearrange("(p j) -> p j", j=COLS)

        def middle_of(b_):
            words = rest[b_][:, :, :, :].rearrange("p g a d -> p (g a d)").bitcast(BF16)
            return words.rearrange("p (g a d w) -> p g a d w", g=2, a=3, w=2)[:, :, :, :, 1]

        def dense_rows(table, m):
            return table[bass.ds(STEP * m, STEP), :].rearrange("(q p t) d -> p q (t d)", q=4, t=2)

        def buf_rows(tile):
            return tile[:, :].rearrange("p (q r) -> p q r", q=4)

        @block.sync
        def _(sp):
            sp.wait_ge(s_pad, 1)
            full = HALF_E // COLS
            for h in range(2):
                sp.dma_start(node_i[64 * h:64 * h + full, :],
                             as_rows(src[h * HALF_E:h * HALF_E + full * COLS])).then_inc(s_src, 16)
                sp.dma_start(node_i[64 * h + full:64 * h + full + 1, 0:HALF_E - full * COLS],
                             as_row(src[h * HALF_E + full * COLS:(h + 1) * HALF_E])).then_inc(s_src, 16)
            sp.dma_start(w1_s[:, :], W1[0:96, :]).then_inc(s_w, 16)
            sp.dma_start(w1u[:, :], W1[96, :].rearrange("(p a) -> p a", a=1)).then_inc(s_w, 16)
            sp.dma_start(b1_s[:, :], b1.rearrange("(p a) -> p a", a=1)).then_inc(s_w, 16)
            sp.dma_start(u_s[:, :], u[0:1, 0].partition_broadcast(P)).then_inc(s_w, 16)
            sp.dma_start(w2_s[:, :], W2).then_inc(s_w, 16)
            sp.dma_start(b2_bc[:, :], b2.partition_broadcast(P)).then_inc(s_w, 16)
            sp.dma_start(w_s[:, :], W).then_inc(s_w, 16)
            sp.dma_start(b_bc[:, :], b.partition_broadcast(P)).then_inc(s_w, 16)
            sp.dma_start(wb_s[D:D + 1, :], as_row(b)).then_inc(s_w, 16)
            sp.wait_ge(s_dpad, 1)
            full = E // COLS
            for t, a in ((dn_i, dst), (ds_i, src)):
                sp.dma_start(t[0:full, :], as_rows(a[0:full * COLS])).then_inc(s_dstl, 16)
                sp.dma_start(t[full:full + 1, 0:E - full * COLS], as_row(a[full * COLS:E])).then_inc(s_dstl, 16)
            sp.dma_start(pair[0:full - 1, :], as_rows(dst[COLS - 1:COLS - 1 + (full - 1) * COLS])[:, 0:2]).then_inc(s_dstl, 16)
            sp.dma_start(pair[full - 1:full, :], as_row(dst[full * COLS - 1:full * COLS + 1])).then_inc(s_dstl, 16)
            sp.wait_ge(s_const, 1)
            for s in range(2):
                sp.dma_start(recs[s][BLOCKS * BLK:, :].rearrange("(p t) r -> p (t r)", t=BT), pad_rec[:, 0:BT * REC]).then_inc(s_tail, 16)
            for t in (T, out):
                sp.dma_start(t[BLOCKS * STEP:ROWS, :].rearrange("(p c) d -> p (c d)", c=SPARE // 96), pad_rec[0:96, 0:SPARE // 96 * D]).then_inc(s_tail, 16)

            def neighbours(side):
                sp.wait_ge(s_line, side + 1)
                sp.dma_start(as_rows(line[side, 1:POS + 1]), nodef[:, :]).then_inc(s_lw, 16)
                sp.dma_start(line[side:side + 1, 0:1], guard[:, 0:1]).then_inc(s_lw, 16)
                sp.dma_start(line[side:side + 1, POS + 1:POS + 2], guard[:, 1:2]).then_inc(s_lw, 16)
                sp.wait_ge(s_lw, 48 * (side + 1))
                sp.dma_start(prev_f[:, :], as_rows(line[side, 0:POS])).then_inc(s_nb, 16)
                sp.dma_start(next_f[:, :], as_rows(line[side, 2:POS + 2])).then_inc(s_nb, 16)

            neighbours(0)
            sp.wait_ge(s_row, 3)
            for r, t in enumerate((tm, tm, hb, td)):
                sp.dma_start(as_rows(rows_src[r]), t[:, :]).then_inc(s_rw, 16)
            sp.wait_ge(s_rw, 64)

            def load_rows(n, b_):
                at = bass.ds(BLK * n, BLK)
                sp.dma_start(c_rows[b_][:, :], rows_src[:, at].unsqueeze(1).to_broadcast([4, FE, BLK])).then_inc(rows_in[b_], 16)

            def next_rows(i, b_):
                sp.wait_ge(feats_ok[b_], i + 1)
                load_rows(2 * i + 2 + b_, b_)

            def store_rec(side, i, b_):
                sp.wait_ge(rec_ok[side][b_], i + 1)
                sp.dma_start(recs[side][bass.ds(BLK * (2 * i + b_), BLK), :].rearrange("(p t) r -> p (t r)", t=BT),
                             rec[b_][:, :, :].rearrange("p t r -> p (t r)")).then_inc(rec_out[side][b_], 16)

            def window(side, j, b_):
                m = 2 * j + b_
                at = [sp.value_load(start_row[side][0:1, bass.ds(2 * m + g, 1)], min_val=0, max_val=E) for g in range(2)]
                stored = [(r_, 16 * (min(c, LOOPS - 1) + 1 if isinstance(c, int) else c + 1))
                          for c, r_ in (back(j, b_, -1), back(j, b_, -2))]
                for r_, count in stored:
                    sp.wait_ge(rec_out[side][r_], count)
                    sp.sem_inc(sp_steps, 1)
                if not isinstance(j, int) or j > 0:
                    sp.wait_ge(rest_ok[side][b_], j)
                for g in range(2):
                    sp.dma_start(win[b_][:, g, :, :], recs[side][bass.ds(at[g], WROWS), :].rearrange("(a p) r -> p a r", p=P)).then_inc(win_in[side][b_], 16)

            def load_dense(side, j, b_, table):
                if not isinstance(j, int) or j > 0:
                    sp.wait_ge(sum_ok[side][b_], j)
                if table is x and isinstance(j, int) and 2 * j + b_ == BLOCKS - 1:
                    left = N - (BLOCKS - 1) * STEP - GROUP
                    sp.dma_start(buf_rows(din[b_])[:, 0:2], x[N - left - GROUP:N - left, :].rearrange("(q p t) d -> p q (t d)", q=2, t=2)).then_inc(d_in[side][b_], 16)
                    sp.dma_start(buf_rows(din[b_])[0:left // 2, 2], x[N - left:N, :].rearrange("(p t) d -> p (t d)", t=2)).then_inc(d_in[side][b_], 16)
                else:
                    sp.dma_start(buf_rows(din[b_]), dense_rows(table, 2 * j + b_)).then_inc(d_in[side][b_], 16)

            def store_dense(side, j, b_, table):
                sp.wait_ge(sum_ok[side][b_], j + 1)
                sp.dma_start(dense_rows(table, 2 * j + b_), buf_rows(dout[b_])).then_inc(d_out[side][b_], 16)

            def turn_src(i, b_, expand=True):
                if expand and some(i, b_, SRC_LAG - 1):
                    window(0, *back(i, b_, SRC_LAG - 1))
                if some(i, b_, -2):
                    next_rows(i, b_)
                if expand and some(i, b_, SRC_LAG + 1):
                    load_dense(0, *back(i, b_, SRC_LAG + 1), x)

            def turn_dst(i, b_, expand=True):
                if expand and some(i, b_, DST_LAG - 1):
                    window(1, *back(i, b_, DST_LAG - 1))
                if some(i, b_, 3):
                    store_rec(1, *back(i, b_, 3))
                if expand and some(i, b_, DST_LAG + 1):
                    load_dense(1, *back(i, b_, DST_LAG + 1), T)
                if expand and some(i, b_, DST_LAG + 3):
                    store_dense(1, *back(i, b_, DST_LAG + 3), out)

            load_rows(0, 0)
            load_rows(1, 1)
            for n in range(SRC_LAG - 1):
                turn_src(n // 2, n % 2)
            sp.wait_ge(s_tail, 64)
            sp.wait_ge(s_fast, 1)
            with sp.If(sp.value_load(fast[0:1, 0:1], min_val=0, max_val=1)):
                turn_src(SRC_LAG // 2 - 1, 1)
                turns(sp, turn_src, SRC_LAG // 2, SRC_LAG)
                for b_ in range(2):
                    sp.wait_ge(d_out[0][b_], 16 * LOOPS)
                sp.sem_inc(table_ok, 1)
                turns(sp, turn_dst, 0, DST_LAG)
                for b_ in range(2):
                    sp.wait_ge(d_out[1][b_], 16 * LOOPS)
            with sp.Else():
                turn_src(SRC_LAG // 2 - 1, 1, expand=False)
                turns(sp, lambda i, b_: turn_src(i, b_, expand=False), SRC_LAG // 2, SRC_LAG)
                for b_ in range(2):
                    sp.wait_ge(rec_out[0][b_], 16 * LOOPS)

                def dense(side, table, to):
                    def step(n):
                        if table is x and isinstance(n, int):
                            left = N - (BLOCKS - 1) * STEP - GROUP
                            sp.dma_start(buf_rows(din[0])[:, 0:2], x[N - left - GROUP:N - left, :].rearrange("(q p t) d -> p q (t d)", q=2, t=2)).then_inc(g_dense_in[side], 16)
                            sp.dma_start(buf_rows(din[0])[0:left // 2, 2], x[N - left:N, :].rearrange("(p t) d -> p (t d)", t=2)).then_inc(g_dense_in[side], 16)
                        else:
                            sp.dma_start(buf_rows(din[0]), dense_rows(table, n)).then_inc(g_dense_in[side], 16)
                        sp.wait_ge(g_dense_ok[side], n + 1)
                        sp.dma_start(dense_rows(to, n), buf_rows(dout[0])).then_inc(g_dense_out[side], 16)
                        sp.wait_ge(g_dense_out[side], 16 * (n + 1))
                        sp.sem_inc(sp_steps, 1)

                    with nc.sync.Fori(0, BLOCKS - 1) as n:
                        step(n)
                    step(BLOCKS - 1)

                def load_records(side):
                    with nc.sync.Fori(0, BLOCKS) as n:
                        sp.dma_start(rec[0][:, :, :].rearrange("p t r -> p (t r)"),
                                     recs[side][bass.ds(BLK * n, BLK), :].rearrange("(p t) r -> p (t r)", t=BT)).then_inc(g_row_in[side], 16)
                        sp.wait_ge(g_sent[side], 16 * BT * (n + 1))
                        sp.sem_inc(sp_steps, 1)

                dense(0, x, T)
                load_records(0)
                sp.wait_ge(g_pad, 1)
                full = HALF_E // COLS
                for h in range(2):
                    sp.dma_start(node_i[64 * h:64 * h + full, :],
                                 as_rows(dst[h * HALF_E:h * HALF_E + full * COLS])).then_inc(g_dst_in, 16)
                    sp.dma_start(node_i[64 * h + full:64 * h + full + 1, 0:HALF_E - full * COLS],
                                 as_row(dst[h * HALF_E + full * COLS:(h + 1) * HALF_E])).then_inc(g_dst_in, 16)
                neighbours(1)
                sp.wait_ge(s_row, 4)
                sp.dma_start(as_rows(rows_dst[0]), tm[:, :]).then_inc(g_rows_stored, 16)
                sp.wait_ge(g_rows_stored, 16)
                dense(1, T, out)
                with nc.sync.Fori(0, BLOCKS) as n:
                    sp.dma_start(c_rows[0][0:D, :], rows_dst[0, bass.ds(BLK * n, BLK)].partition_broadcast(D)).then_inc(g_c, 16)
                    sp.wait_ge(g_rec, n + 1)
                    sp.dma_start(recs[1][bass.ds(BLK * n, BLK), :].rearrange("(p t) r -> p (t r)", t=BT),
                                 rec[0][:, :, :].rearrange("p t r -> p (t r)")).then_inc(g_stored, 16)
                    sp.wait_ge(g_stored, 16 * (n + 1))
                    sp.sem_inc(sp_steps, 1)
                load_records(1)

        @block.gpsimd
        def _(pool):
            g = nc.gpsimd
            step = [0]

            def link(ins):
                step[0] += 1
                ins.then_inc(s_pool, 1)
                pool.wait_ge(s_pool, step[0])

            link(g.iota(pos_i[:, :], [[1, COLS]], base=0, channel_multiplier=COLS))
            link(g.iota(psign_i[:, :], [[1, 1]], base=0, channel_multiplier=1))
            link(g.iota(prow_i[:, :], [[1, P]], base=0, channel_multiplier=0))
            link(g.memset(dn_i[:, :], PAD))
            g.memset(ds_i[:, :], 0).then_inc(s_dpad, 1)
            pool.wait_ge(s_dpad, 1)
            link(g.iota(node_i16[:, :], [[2 * P, 2], [1, 2], [2, P]], base=0, channel_multiplier=0))
            link(g.iota(base_i[:, :], [[GROUP, GROUPS]], base=0, channel_multiplier=0))
            link(g.iota(limit_i[:, :], [[BLK, GROUPS // 2], [0, 2]], base=3 * BLK, channel_multiplier=0))
            link(g.tensor_copy(node_of[:, :], node_i16[:, :]))
            link(g.tensor_copy(base_f[:, :], base_i[:, :]))
            link(g.tensor_copy(limit[:, :], limit_i[:, :]))
            link(g.tensor_scalar(span_f[:, :], prow_i[:, 0:SPAN], float(GROUP), GROUP - 0.5, ALU.mult, ALU.add))
            link(g.memset(guard[:, :], -1.0))
            link(g.memset(eps_t[:, :], EPS))
            link(g.memset(one[:, :], 1.0))
            link(g.memset(one_b[:, :], 1.0))
            link(g.memset(wrong[:, :], 0.0))
            link(g.memset(pad_rec[:, :], -1.0))
            for b_ in range(2):
                link(g.memset(agg[b_][D:D + 1, :], 1.0))
                link(g.memset(rec[b_][:, :, :], 0.0))
            link(g.memset(ident[:, :], 0.0))
            link(g.memset(less[:, 0:1], 0.0))
            g.affine_select(out=ident[:, :], in_=ident[:, :], compare_op=ALU.not_equal, fill=1.0, base=0,
                                 pattern=[[-1, P]], channel_multiplier=1).then_inc(s_const, 1)
            pool.wait_ge(s_const, 1)

            pool.wait_ge(s_dstl, 96)
            link(g.tensor_copy(dn_f[:, :], dn_i[:, :]))
            g.tensor_copy(ds_f[:, :], ds_i[:, :]).then_inc(s_dplane, 1)
            pool.wait_ge(s_dplane, 1)
            pool.wait_ge(s_idx, 1)

            def gather_attr(i, b_):
                pool.wait_ge(staged[b_], i + 1)
                pool.sem_inc(pool_blocks, 1)
                for t in range(BT):
                    g.indirect_dma_start(
                        out=attr[b_][:, t, :], out_offset=None, in_=edge_attr,
                        in_offset=bass.IndirectOffsetOnAxis(ap=stage_i[b_][:, t:t + 1], axis=0)).then_inc(gathered[b_], 16)

            def gather_x(i, b_):
                pool.wait_ge(staged2[b_], i + 1)
                pool.sem_inc(pool_blocks, 1)
                for t in range(BT):
                    g.indirect_dma_start(
                        out=xg[b_][:, t, :], out_offset=None, in_=T,
                        in_offset=bass.IndirectOffsetOnAxis(ap=stage_i[b_][:, t:t + 1], axis=0)).then_inc(gathered2[b_], 16)

            with g.Fori(0, LOOPS) as i:
                gather_attr(i, 0)
                gather_attr(i, 1)
            pool.wait_ge(s_fast, 1)
            with pool.If(pool.value_load(fast[0:1, 0:1], min_val=0, max_val=1)):
                pool.wait_ge(table_ok, 1)
                with g.Fori(0, LOOPS) as i:
                    gather_x(i, 0)
                    gather_x(i, 1)
            with pool.Else():
                def scatter(side, table):
                    with g.Fori(0, BLOCKS) as n:
                        pool.wait_ge(g_row_in[side], 16 * (n + 1))
                        pool.sem_inc(pool_blocks, 1)
                        pool.wait_ge(g_row_ok[side], n + 1)
                        pool.sem_inc(pool_blocks, 1)
                        for t in range(BT):
                            g.indirect_dma_start(
                                out=table, out_offset=bass.IndirectOffsetOnAxis(ap=stage_i[0][:, t:t + 1], axis=0),
                                in_=rec[0][:, t, 0:D], in_offset=None, compute_op=ALU.add).then_inc(g_sent[side], 16)
                    pool.wait_ge(g_sent[side], 16 * BT * BLOCKS)

                scatter(0, T)
                with g.Fori(0, BLOCKS) as n:
                    pool.wait_ge(g_edge, n + 1)
                    pool.sem_inc(pool_blocks, 1)
                    for t in range(BT):
                        g.indirect_dma_start(
                            out=source_i[:, t:t + 1], out_offset=None, in_=src.rearrange("(e a) -> e a", a=1),
                            in_offset=bass.IndirectOffsetOnAxis(ap=stage_i[0][:, t:t + 1], axis=0)).then_inc(g_source, 16)
                    pool.wait_ge(g_source, 16 * BT * (n + 1))
                    pool.sem_inc(pool_blocks, 1)
                    for t in range(BT):
                        g.indirect_dma_start(
                            out=xg[0][:, t, :], out_offset=None, in_=T,
                            in_offset=bass.IndirectOffsetOnAxis(ap=source_i[:, t:t + 1], axis=0)).then_inc(g_x, 16)
                scatter(1, out)

        @block.scalar
        def _(act):
            s = nc.scalar
            def count_below(plane):
                for k in range(SPAN):
                    last = s.activation(sign_out[:, :], plane[:, :], ACT.Sign, bias=bound[:, k:k + 1], scale=-1.0,
                                        accum_out=signs[:, k:k + 1])
                    if k < SPAN - 1:
                        last.then_inc(s_signs, 1)
                        act.wait_ge(s_signs, sides[0] * SPAN + k + 1)
                last.then_inc(s_signs, 1)
                sides[0] += 1

            sides = [0]
            act.wait_ge(s_dplane, 1)
            act.wait_ge(s_bound, 1)
            count_below(dn_f)
            act.wait_ge(s_dturn, 1)
            for to, of in ((gi[1], p_z[0]), (rn[1], p_z[1])):
                last = s.copy(to[:, :].rearrange("c (n t) -> c t n", t=BT), of[:, :].rearrange("c (t n) -> c t n", n=P))
            last.then_inc(s_dcols, 1)
            act.wait_ge(s_wts, 1)
            act.wait_ge(s_bound, 2)
            count_below(nodef)
            act.wait_ge(s_idx, 1)

            def triple(i, b_):
                act.wait_ge(gathered[b_], 16 * BT * (i + 1))
                s.copy(attr3[b_][:, :, 0:2, :], attr[b_][:, :, :].unsqueeze(2).to_broadcast([P, BT, 2, FE]))
                for t in range(BT):
                    last = s.activation(attr3[b_][:, t, 2, :], attr[b_][:, t, :], ACT.Copy,
                                        scale=share[:, bass.ds(BT * (2 * i + b_) + t, 1)])
                last.then_inc(tripled[b_], 1)

            def hidden(i, b_):
                act.wait_ge(z_ok[b_], i + 1)
                s.activation(hid[b_][:, :], p_z[b_][:, :], ACT.Relu, bias=bias_z[:, :]).then_inc(hid_ok[b_], 1)

            def record(side, made, i, b_):
                act.wait_ge(made[b_], i + 1)
                if not isinstance(i, int) or i > 0:
                    act.wait_ge(rec_out[side][b_], 16 * i)
                s.copy(rec[b_][:, :, D], rn[side][:, bass.ds(BT * (2 * i + b_), BT)])
                s.copy(rec[b_][:, :, 0:D], p_m[b_][:, :, 0:D]).then_inc(rec_ok[side][b_], 1)

            def store_rec(side, i, b_):
                act.wait_ge(rec_ok[side][b_], i + 1)
                s.dma_start(recs[side][bass.ds(BLK * (2 * i + b_), BLK), :].rearrange("(p t) r -> p (t r)", t=BT),
                            rec[b_][:, :, :].rearrange("p t r -> p (t r)")).then_inc(rec_out[side][b_], 16)

            def store_dense(side, j, b_, table):
                act.wait_ge(sum_ok[side][b_], j + 1)
                s.dma_start(dense_rows(table, 2 * j + b_), buf_rows(dout[b_])).then_inc(d_out[side][b_], 16)

            def upper(side, j, b_):
                act.wait_ge(win_in[side][b_], 32 * (j + 1))
                if not isinstance(j, int) or j > 0:
                    act.wait_ge(exp_ok[side][b_], j)
                s.copy(upper_b[b_][:, :, :, :], win[b_][:, :, :, 0:D]).then_inc(hi_ok[side][b_], 1)

            def turn_src(i, b_, expand=True):
                if expand and some(i, b_, SRC_LAG - 1):
                    upper(0, *back(i, b_, SRC_LAG - 1))
                if some(i, b_, -2):
                    triple(*back(i, b_, -2))
                if some(i, b_, -1):
                    hidden(*back(i, b_, -1))
                if some(i, b_, 0):
                    record(0, m_ok, i, b_)
                if expand and some(i, b_, SRC_LAG + 2):
                    store_dense(0, *back(i, b_, SRC_LAG + 2), T)
                if some(i, b_, 0):
                    store_rec(0, i, b_)

            triple(0, 0)
            triple(0, 1)
            hidden(0, 0)
            for n in range(SRC_LAG - 1):
                turn_src(n // 2, n % 2)

            def copy_x(i, b_):
                act.wait_ge(gathered2[b_], 16 * BT * (i + 1))
                if not isinstance(i, int) or i > 0:
                    act.wait_ge(h_ok[b_], i)
                s.copy(x1[b_][:, :, :], xg[b_][:, :, :]).then_inc(copied[b_], 1)

            def deviation(i, b_):
                act.wait_ge(var_ok[b_], i + 1)
                s.activation(sd[b_][:, :], mv[b_][:, :, 1], ACT.Sqrt, bias=eps_t[:, :]).then_inc(sd_ok[b_], 1)

            def normalize(i, b_):
                act.wait_ge(norm_ok[b_], i + 1)
                for t in range(BT):
                    last = s.activation(hn[b_][:, t, :], x1[b_][:, t, :], ACT.Relu,
                                        bias=nmr[b_][:, t:t + 1], scale=rstd[b_][:, t:t + 1])
                last.then_inc(h_ok[b_], 1)

            def take_turned(i, b_):
                act.wait_ge(ht_ok[b_], i + 1)
                s.copy(agg[b_][0:D, :], p_g[b_][0:D, :]).then_inc(hts_ok[b_], 1)

            act.wait_ge(s_fast, 1)
            with act.If(act.value_load(fast[0:1, 0:1], min_val=0, max_val=1)):
                turn_src(SRC_LAG // 2 - 1, 1)
                turns(s, turn_src, SRC_LAG // 2, SRC_LAG)

                def turn_dst(i, b_):
                    if some(i, b_, DST_LAG):
                        upper(1, *back(i, b_, DST_LAG))
                    if some(i, b_, 0):
                        deviation(i, b_)
                    if some(i, b_, -1):
                        copy_x(*back(i, b_, -1))
                    if some(i, b_, 0):
                        normalize(i, b_)
                    if some(i, b_, 1):
                        take_turned(*back(i, b_, 1))
                    if some(i, b_, 2):
                        record(1, y_ok, *back(i, b_, 2))

                for b_ in range(2):
                    act.wait_ge(rec_out[0][b_], 16 * LOOPS)
                copy_x(0, 0)
                turns(s, turn_dst, 0, DST_LAG)
            with act.Else():
                turn_src(SRC_LAG // 2 - 1, 1, expand=False)
                turns(s, lambda i, b_: turn_src(i, b_, expand=False), SRC_LAG // 2, SRC_LAG)
                with s.Fori(0, BLOCKS) as n:
                    act.wait_ge(g_var, n + 1)
                    s.activation(sd[0][:, :], mv[0][:, :, 1], ACT.Sqrt, bias=eps_t[:, :]).then_inc(g_sd, 1)
                    act.wait_ge(g_norm, n + 1)
                    for t in range(BT):
                        last = s.activation(hn[0][:, t, :], xg[0][:, t, :], ACT.Relu,
                                            bias=nmr[0][:, t:t + 1], scale=rstd[0][:, t:t + 1])
                    last.then_inc(g_h, 1)

        @block.vector
        def _(dve):
            step = [0]
            v = nc.vector

            def link(ins):
                step[0] += 1
                ins.then_inc(s_v, 1)
                dve.wait_ge(s_v, step[0])

            v.memset(node_i[:, :], PAD).then_inc(s_pad, 1)
            dve.wait_ge(s_pool, 3)
            v.tensor_copy(pos_f[:, :], pos_i[:, :])
            v.tensor_scalar(low_i[:, :], pos_i[:, :], 2 ** LOW - 1, None, ALU.bitwise_and)
            link(v.tensor_scalar(srcs_i[:, :], pos_i[:, :], DUMMY - 1, None, ALU.bitwise_and))
            v.tensor_scalar(dummy_f[:, :], srcs_i[:, :], float(N), None, ALU.add)
            link(v.tensor_scalar(psign_i[:, :], psign_i[:, :], 1, None, ALU.bitwise_and))
            link(v.tensor_scalar(psign[:, :], psign_i[:, :], -2.0, 1.0, ALU.mult, ALU.add))
            for m in range(7):
                link(v.tensor_scalar(bit_a[:, :], prow_i[:, :], m, 1, ALU.logical_shift_right, ALU.bitwise_and))
                if m < 6:
                    link(v.tensor_scalar(bit_b[:, :], prow_i[:, :], m + 1, 1, ALU.logical_shift_right, ALU.bitwise_and))
                    link(v.tensor_tensor(bit_a[:, :], bit_a[:, :], bit_b[:, :], ALU.bitwise_xor))
                else:
                    link(v.tensor_copy(bit_b[:, :], bit_a[:, :]))
                    for q in range(BT):
                        v.tensor_copy(ha[:, q * P:(q + 1) * P], bit_b[:, :])
                link(v.tensor_scalar(flip[:, m, :], bit_a[:, :], -2.0, 1.0, ALU.mult, ALU.add))
            dve.wait_ge(s_w, 144)
            link(v.scalar_tensor_tensor(bias_z[:, :], w1u[:, :], u_s[:, 0:1], b1_s[:, :], ALU.mult, ALU.add))
            v.tensor_scalar(r0[:, :], bias_z[:, :].to_broadcast([P, P]), 0.0, None, ALU.max).then_inc(s_r0, 1)
            v.tensor_scalar(relub[:, :], b_bc[:, :], 0.0, None, ALU.max)
            dve.wait_ge(s_pw, 1)
            v.tensor_scalar(c_neg[:, :], p_t[:, 0:D], -1.0, None, ALU.mult)
            v.tensor_copy(wb_s[0:D, :], p_u[0:D, 0:D])
            link(v.tensor_tensor(c_bc[:, :], p_t[:, 0:D], b2_bc[:, :], ALU.add))

            def three_parts(row, to):
                link(v.tensor_copy(part_b[0][:, :], row[:, :]))
                link(v.tensor_tensor(part_f[0][:, :], row[:, :], part_b[0][:, :], ALU.subtract))
                link(v.tensor_copy(part_b[1][:, :], part_f[0][:, :]))
                link(v.tensor_tensor(part_f[1][:, :], part_f[0][:, :], part_b[1][:, :], ALU.subtract))
                link(v.tensor_scalar(part_f[1][:, :], part_f[1][:, :], ident[:, 2:3], None, ALU.mult))
                link(v.scalar_tensor_tensor(part_f[2][:, :], part_b[1][:, :], ident[:, 1:2], part_f[1][:, :], ALU.mult, ALU.add))
                link(v.scalar_tensor_tensor(part_f[1][:, :], part_b[0][:, :], ident[:, 0:1], part_f[2][:, :], ALU.mult, ALU.add))
                for q in range(to.shape[1]):
                    last = v.tensor_copy(to[:, q, :], part_f[1][:, :])
                link(last)

            dve.wait_ge(s_const, 1)
            three_parts(c_neg, nc3)
            three_parts(c_bc, c3[0])
            three_parts(b_bc, c3[1])
            v.tensor_copy(rowmax[:, :], eps_t[:, :]).then_inc(s_wts, 1)

            def bounds(first_node_i):
                link(v.tensor_scalar(low_node_i[:, 0:1], first_node_i, 9, 9, ALU.logical_shift_right, ALU.logical_shift_left))
                link(v.tensor_copy(low_node[:, :], low_node_i[:, 0:1]))
                v.tensor_scalar(bound[:, :], span_f[:, :], low_node[:, 0:1], None, ALU.add).then_inc(s_bound, 1)
                sides[0] += 1

            def rows_above():
                dve.wait_ge(s_bound, sides[0])
                for k in range(SPAN):
                    v.tensor_scalar(above[:, k, :], base_f[:, :], bound[:, k:k + 1], None, ALU.is_gt)
                dve.wait_ge(s_signs, SPAN * sides[0])
                link(v.tensor_scalar(less[:, 1:SPAN + 1], signs[:, :], 0.5, COLS / 2, ALU.mult, ALU.add))
                v.tensor_tensor(in_group[:, :], less[:, 1:SPAN + 1], less[:, 0:SPAN], ALU.subtract).then_inc(s_above, 1)

            def group_starts(side):
                dve.wait_ge(s_base, sides[0])
                link(v.tensor_copy(start_f[:, :], p_s[0:1, 256 * side:256 * side + GROUPS]))
                v.tensor_copy(start_row[side][:, :], start_f[:, :])
                last = 2 * BLOCKS
                link(v.tensor_tensor(over[:, 0:last], start_f[:, 1:last + 1], start_f[:, 0:last], ALU.subtract))
                v.tensor_scalar(over[:, 0:last], over[:, 0:last], float(WROWS), None, ALU.is_gt)
                link(v.scalar_tensor_tensor(over2[:, 0:last], start_f[:, 0:last], float(WROWS), limit[0:1, 0:last], ALU.add, ALU.is_gt))
                link(v.tensor_tensor(over[:, 0:last], over[:, 0:last], over2[:, 0:last], ALU.add))
                v.reduce_sum(wrong[0:1, side:side + 1], over[:, 0:last], AX.X)
                link(v.tensor_scalar(wrong[0:1, 4 + side:5 + side], start_f[:, last:last + 1], float(E), None, ALU.not_equal))

            sides = [0]

            def beside_turn(t):
                if t == 0:
                    dve.wait_ge(s_dstl, 96)
                    bounds(dn_i[:, 0:1])
                elif t == 1:
                    dve.wait_ge(s_dplane, 1)
                    link(v.tensor_tensor(prev_f[:, 1:COLS], dn_f[:, 1:COLS], dn_f[:, 0:COLS - 1], ALU.is_lt))
                elif t == 2:
                    rows_above()
                elif t == 3:
                    link(v.reduce_sum(wrong[:, 2:3], prev_f[:, 1:COLS], AX.X))
                elif t == 6:
                    full = E // COLS
                    v.tensor_tensor(wrong[0:full, 3:4], pair[0:full, 1:2], pair[0:full, 0:1], ALU.is_lt)
                    group_starts(1)

            def encode():
                v.tensor_scalar(tm[:, :], node_i[:, :], float(SPLIT), None, ALU.is_ge)
                link(v.tensor_scalar(td[:, :], node_i[:, :], 2.0, float(HIGH_ADD - LOW_TOP), ALU.mult, ALU.add))
                link(v.tensor_tensor(tm[:, :], tm[:, :], td[:, :], ALU.mult))
                link(v.tensor_scalar(td[:, :], node_i[:, :], -1.0, float(LOW_TOP), ALU.mult, ALU.add))
                link(v.tensor_tensor(kb[:, :].bitcast(I32), td[:, :], tm[:, :], ALU.add))
                link(v.tensor_scalar(kb[:, :].bitcast(I32), kb[:, :].bitcast(I32), LOW, None, ALU.logical_shift_left))
                link(v.tensor_tensor(ka[:, :].bitcast(I32), kb[:, :].bitcast(I32), low_i[:, :], ALU.bitwise_or))
                link(v.tensor_scalar(kb[:, :], ka[:, :], psign[:, :], None, ALU.mult))

            def pairs(tile, d):
                w = tile[:, :].rearrange("p (n t d) -> p n t d", t=2, d=d)
                return w[:, :, 0, :], w[:, :, 1, :]

            def mirror(tile, m):
                w = tile[:, :].rearrange("p (n m) -> p n m", m=m)
                return w[:, :, 0:m // 2], w[:, :, m // 2:m][:, :, ::-1]

            def sort(to_turn, turned_by, beside=lambda t: None):
                keys = [kb, ka]
                half = [ha, hb]

                def finish(ins, last):
                    if last:
                        ins.then_inc(to_turn, 1)
                    else:
                        link(ins)

                def exchange(view, arg, of=None, last=False):
                    lo, hi = view(keys[0] if of is None else of, arg)
                    to_lo, to_hi = view(keys[1], arg)
                    if of is not None:
                        link(v.tensor_copy(to_hi, hi))
                        hi = to_hi
                    v.tensor_tensor(to_lo, lo, hi, ALU.max)
                    finish(v.tensor_tensor(to_hi, lo, hi, ALU.min), last)
                    keys.reverse()

                def exchange_halves(d, of=None, half_of=None, last=False):
                    lo, hi = pairs(keys[0] if of is None else of, d)
                    to_lo, to_hi = pairs(keys[1], d)
                    hlo, hhi = pairs(half[0] if half_of is None else half_of, d)
                    to_hlo, to_hhi = pairs(half[1], d)
                    if of is not None:
                        v.tensor_copy(to_hi, hi)
                        link(v.tensor_copy(to_hhi, hhi))
                        hi, hhi = to_hi, to_hhi
                    first, _ = pairs(tm, d)
                    apart, _ = pairs(td, d)
                    v.tensor_tensor(first, lo, hi, ALU.is_ge)
                    link(v.tensor_tensor(apart, hlo, hhi, ALU.subtract))
                    v.tensor_tensor(to_lo, lo, hi, ALU.max)
                    v.tensor_tensor(to_hi, lo, hi, ALU.min)
                    link(v.tensor_tensor(first, first, apart, ALU.mult))
                    low_half = v.tensor_tensor(to_hlo, hhi, first, ALU.add)
                    if of is not None:
                        link(low_half)
                    finish(v.tensor_tensor(to_hhi, hlo, first, ALU.subtract), last)
                    keys.reverse()
                    half.reverse()

                for k in range(1, 10):
                    exchange(mirror, 2 ** k)
                    for q in range(k - 2, -1, -1):
                        exchange(pairs, 2 ** q, last=(k == 9 and q == 0))
                for k in range(10, 17):
                    assert keys[0] is key_tiles[turn_from[2 * (k - 10)]]
                    beside(2 * (k - 10))
                    dve.wait_ge(turned_by, 2 * (k - 10) + 1)
                    link(v.tensor_tensor(keys[1][:, :].rearrange("c (b p) -> c b p", p=P),
                                         p_t[:, :].rearrange("c (b p) -> c b p", p=P),
                                         flip[:, k - 10:k - 9, :].to_broadcast([P, BT, P]), ALU.mult))
                    keys.reverse()
                    for q in range(k - 10, -1, -1):
                        if k < 16:
                            exchange(pairs, 2 ** q, last=q == 0)
                        else:
                            exchange_halves(2 ** q, last=q == 0)
                    assert keys[0] is key_tiles[turn_from[2 * (k - 10) + 1]]
                    beside(2 * (k - 10) + 1)
                    dve.wait_ge(turned_by, 2 * (k - 10) + 2)
                    for q in range(8, -1, -1):
                        of = p_t if q == 8 else None
                        if k < 16:
                            exchange(pairs, 2 ** q, of=of, last=q == 0)
                        else:
                            exchange_halves(2 ** q, of=of, half_of=p_u if q == 8 else None)
                assert keys[0] is sorted_in and half[0] is ha

            def decode(ready):
                v.tensor_scalar(srcs_i[:, :], sorted_in[:, :].bitcast(I32), 2 ** LOW - 1, None, ALU.bitwise_and)
                link(v.tensor_scalar(node_i[:, :].bitcast(U32), sorted_in[:, :].bitcast(U32), LOW, None, ALU.logical_shift_right))
                v.tensor_scalar(tm[:, :], node_i[:, :], float(2 ** 16), None, ALU.is_ge)
                link(v.tensor_scalar(td[:, :], node_i[:, :], 2.0, -float(HIGH_ADD + LOW_TOP), ALU.mult, ALU.add))
                v.tensor_tensor(td[:, :], td[:, :], tm[:, :], ALU.mult)
                link(v.tensor_scalar(nodef[:, :], node_i[:, :], -1.0, float(LOW_TOP), ALU.mult, ALU.add))
                v.tensor_tensor(nodef[:, :], nodef[:, :], td[:, :], ALU.add).then_inc(s_line, 1)
                link(v.scalar_tensor_tensor(gidx_f[:, :], ha[:, :], float(HALF_E), srcs_i[:, :], ALU.mult, ALU.add))
                link(v.tensor_scalar(gidx_f[:, :], gidx_f[:, :], float(E - 1), None, ALU.min))

            turned_n = [14, 14]

            def to_columns(tile, turned_):
                return v.tensor_copy(tile[:, :].rearrange("c (n t) -> c t n", t=BT),
                                     turned_[:, :].rearrange("c (t n) -> c t n", n=P))

            def prepare(side, ka, kb):
                dve.wait_ge(s_nb, 32 * (side + 1))
                v.tensor_tensor(tm[:, :], nodef[:, :], prev_f[:, :], ALU.is_equal).then_inc(s_row, 1)
                dve.wait_ge(s_row, 1 + 3 * side)
                if side == 0:
                    link(v.tensor_scalar(td[:, :], tm[:, :], 2.0, -1.0, ALU.mult, ALU.add))
                    link(v.tensor_scalar(kb[:, :], tm[:, :], -1.0, 1.0, ALU.mult, ALU.add))
                    v.tensor_scalar(td[:, :], td[:, :], BIG, None, ALU.mult).then_inc(s_row, 1)
                    link(v.tensor_tensor(kb[:, :], kb[:, :], pos_f[:, :], ALU.mult))
                    v.reduce_max(rowmax[:, :], kb[:, :], AX.X).then_inc(s_tt[side], 1)
                    link(v.memset(pmax[:, 0:1], 0.0))
                    turned_n[side] += 1
                    dve.wait_ge(s_pt[side], turned_n[side])
                    link(v.tensor_copy(prev_f[0:1, 0:P], p_u[0:1, 0:P]))
                    v.tensor_tensor_scan(pmax[0:1, 1:P + 1], prev_f[0:1, 0:P], prev_f[0:1, 0:P], 0.0,
                                         ALU.max, ALU.max).then_inc(s_tt[side], 1)
                    turned_n[side] += 1
                    dve.wait_ge(s_pt[side], turned_n[side])
                    link(v.tensor_copy(carry_p[:, :], p_u[:, 256:257]))
                    link(v.tensor_tensor_scan(ka[:, :], kb[:, :], kb[:, :], carry_p[:, 0:1], ALU.max, ALU.max))
                    link(v.scalar_tensor_tensor(kb[:, :], ka[:, :], -1.0, pos_f[:, :], ALU.mult, ALU.add))
                    link(v.tensor_scalar(kb[:, :], kb[:, :], 1.0, None, ALU.add))
                    link(v.reciprocal(ha[:, :], kb[:, :]))
                    v.tensor_scalar(hb[:, :], ha[:, :], -1.0, 1.0, ALU.mult, ALU.add).then_inc(s_row, 1)
                    dve.wait_ge(s_row, 3)
                v.tensor_tensor(kb[:, :], nodef[:, :], next_f[:, :], ALU.not_equal)
                link(v.tensor_tensor(ka[:, :], nodef[:, :], dummy_f[:, :], ALU.subtract))
                v.tensor_tensor(ka[:, :], ka[:, :], kb[:, :], ALU.mult)
                link(v.scalar_tensor_tensor(kb[:, :], nodef[:, :], 1.0, kb[:, :], ALU.add, ALU.mult))
                v.tensor_scalar(kb[:, :], kb[:, :], -1.0, None, ALU.add)
                v.tensor_tensor(ka[:, :], ka[:, :], dummy_f[:, :], ALU.add).then_inc(s_tt[side], 1)
                turned_n[side] += 1
                dve.wait_ge(s_pt[side], turned_n[side])
                to_columns(gi[side], p_t)
                to_columns(sx, p_u).then_inc(s_tt[side], 1)
                turned_n[side] += 1
                dve.wait_ge(s_pt[side], turned_n[side])
                if side == 0:
                    to_columns(share, p_u)
                to_columns(rn[side], p_t).then_inc(s_idx, 1)

            dve.wait_ge(s_src, 64)
            encode()
            sort(s_tt[0], s_pt[0], beside_turn)
            decode(s_line)
            link(v.tensor_copy(low_node_i[:, 1:2], nodef[:, 0:1]))
            bounds(low_node_i[:, 1:2])
            prepare(0, sorted_in, spare)

            def stage(n, b_, side, ok):
                v.tensor_copy(stage_i[b_][:, :], gi[side][:, bass.ds(BT * n, BT)]).then_inc(ok[b_], 1)

            dve.wait_ge(s_idx, 1)
            for b_ in range(2):
                stage(b_, b_, 0, staged)

            rows_above()
            group_starts(0)
            v.reduce_sum(wrong1[:, :], wrong[:, :], AX.X).then_inc(s_wrong, 1)
            dve.wait_ge(s_wsum, 1)
            v.tensor_scalar(fast[:, :], p_s[0:1, COLS - 1:COLS], 0.0, None, ALU.is_equal).then_inc(s_fast, 1)

            link(v.memset(carry[:, :], 0.0))

            def scans(i, b_):
                n = 2 * i + b_
                dve.wait_ge(turned[b_], i + 1)
                if some(i, b_, -2):
                    stage(n + 2, b_, 0, staged)
                dve.wait_ge(rows_in[b_], 16 * (i + 1))
                if not (isinstance(n, int) and n == 0):
                    dve.wait_ge(carried, n)
                f, c = feats[b_], c_rows[b_]
                v.tensor_tensor_scan(f[0:96, :], c[0:96, :], p_g[b_][0:96, :], carry[0:96, 0:1],
                                     ALU.mult, ALU.add).then_inc(summed, 1)

            def maximum(i, b_):
                n = 2 * i + b_
                f, c = feats[b_], c_rows[b_]
                dve.wait_ge(summed, n + 1)
                v.tensor_tensor_scan(f[32:64, :], c[96:128, :], p_g[b_][32:64, :], carry[32:64, 0:1],
                                     ALU.min, ALU.max).then_inc(feats_ok[b_], 1)

            def carry_on(i, b_):
                n = 2 * i + b_
                dve.wait_ge(feats_ok[b_], i + 1)
                v.tensor_copy(carry[:, :], feats[b_][:, BLK - 1:BLK]).then_inc(carried, 1)

            def relative(side, j, b_):
                m = 2 * j + b_
                dve.wait_ge(win_in[side][b_], 32 * (j + 1))
                v.tensor_tensor(rel[b_][:, :, :], win[b_][:, :, :, D],
                                base_f[:, bass.ds(2 * m, 2)].unsqueeze(2).to_broadcast([P, 2, 3]),
                                ALU.subtract).then_inc(rel_ok[side][b_], 1)

            def onehots(side, j, b_):
                if not isinstance(j, int) or j > 0:
                    dve.wait_ge(exp_ok[side][b_], j)
                dve.wait_ge(rel_ok[side][b_], j + 1)
                for g in range(2):
                    for a in range(3):
                        lo, w = (512 * a, 512) if a < 2 else (1024, 256)
                        v.tensor_scalar(oneh[b_][:, g, lo:lo + w], node_of[:, GROUP - w:GROUP],
                                        rel[b_][:, g, a:a + 1], None, ALU.is_equal)
                dve.wait_ge(hi_ok[side][b_], j + 1)
                v.tensor_tensor(rest[b_][:, :, :, :], win[b_][:, :, :, 0:D], upper_b[b_][:, :, :, :],
                                ALU.subtract).then_inc(rest_ok[side][b_], 1)

            def lower(side, j, b_):
                dve.wait_ge(rest_ok[side][b_], j + 1)
                v.tensor_tensor(lower_b[b_][:, :, :, :], rest[b_][:, :, :, :], middle_of(b_), ALU.subtract).then_inc(lo_ok[side][b_], 1)

            def add_dense(side, j, b_):
                end = isinstance(j, int) and 2 * j + b_ == BLOCKS - 1 and side == 0
                dve.wait_ge(exp_ok[side][b_], j + 1)
                dve.wait_ge(d_in[side][b_], 16 * (j + 1) + (16 if end else 0))
                if not isinstance(j, int) or j > 0:
                    dve.wait_ge(d_out[side][b_], 16 * j)
                if side == 0:
                    ins = v.tensor_tensor(dout[b_][:, :], p_e[b_][:, :], din[b_][:, :], ALU.add)
                else:
                    ins = v.scalar_tensor_tensor(dout[b_][:, :], p_e[b_][:, :], 0.0, din[b_][:, :], ALU.max, ALU.add)
                ins.then_inc(sum_ok[side][b_], 1)

            def turn_src(i, b_, expand=True):
                if some(i, b_, 0):
                    scans(i, b_)
                if expand and some(i, b_, SRC_LAG):
                    relative(0, *back(i, b_, SRC_LAG))
                if some(i, b_, 0):
                    maximum(i, b_)
                if expand and some(i, b_, SRC_LAG):
                    onehots(0, *back(i, b_, SRC_LAG))
                if some(i, b_, 0):
                    carry_on(i, b_)
                if expand and some(i, b_, SRC_LAG + 2):
                    add_dense(0, *back(i, b_, SRC_LAG + 2))
                if expand and some(i, b_, SRC_LAG):
                    lower(0, *back(i, b_, SRC_LAG))

            for n in range(SRC_LAG):
                turn_src(n // 2, n % 2)
            dve.wait_ge(s_fast, 1)
            links = step[0]
            with dve.If(dve.value_load(fast[0:1, 0:1], min_val=0, max_val=1)):
                turns(v, turn_src, SRC_LAG // 2, SRC_LAG)
                dve.wait_ge(s_dcols, 1)
                for b_ in range(2):
                    stage(b_, b_, 1, staged2)

                def moments(i, b_):
                    dve.wait_ge(copied[b_], i + 1)
                    if some(i, b_, -2):
                        stage(2 * i + 2 + b_, b_, 1, staged2)
                    for t in range(BT):
                        last = v.bn_stats(stat[b_][:, t, :], x1[b_][:, t, :])
                    last.then_inc(stat_ok[b_], 1)
                    dve.wait_ge(stat_ok[b_], i + 1)
                    v.tensor_copy(rowmax[:, :], eps_t[:, :])
                    for t in range(BT):
                        last = v.bn_aggr(mv[b_][:, t, :], stat[b_][:, t, :])
                    last.then_inc(var_ok[b_], 1)

                def norm(i, b_):
                    dve.wait_ge(sd_ok[b_], i + 1)
                    v.reciprocal(rstd[b_][:, :], sd[b_][:, :]).then_inc(rstd_ok[b_], 1)
                    dve.wait_ge(rstd_ok[b_], i + 1)
                    v.scalar_tensor_tensor(nmr[b_][:, :], mv[b_][:, :, 0], -1.0, rstd[b_][:, :],
                                           ALU.mult, ALU.mult).then_inc(norm_ok[b_], 1)

                def turn_dst(i, b_):
                    if some(i, b_, 0):
                        moments(i, b_)
                    if some(i, b_, DST_LAG):
                        relative(1, *back(i, b_, DST_LAG))
                        onehots(1, *back(i, b_, DST_LAG))
                    if some(i, b_, 0):
                        norm(i, b_)
                    if some(i, b_, DST_LAG + 2):
                        add_dense(1, *back(i, b_, DST_LAG + 2))
                    if some(i, b_, DST_LAG):
                        lower(1, *back(i, b_, DST_LAG))

                turns(v, turn_dst, 0, DST_LAG)
            with dve.Else():
                step[0] = links
                turns(v, lambda i, b_: turn_src(i, b_, expand=False), SRC_LAG // 2, SRC_LAG)

                def dense(side, row):
                    def step(n, parts=1):
                        dve.wait_ge(g_dense_in[side], 16 * (n + parts))
                        v.tensor_tensor(dout[0][:, :].rearrange("p (q d) -> p q d", d=D),
                                        din[0][:, :].rearrange("p (q d) -> p q d", d=D),
                                        row[:, :].unsqueeze(1).to_broadcast([P, 2 * BT, D]), ALU.add).then_inc(g_dense_ok[side], 1)
                        dve.wait_ge(g_dense_out[side], 16 * (n + 1))
                        v.tensor_copy(rowmax[:, :], eps_t[:, :])

                    with v.Fori(0, BLOCKS - 1) as n:
                        step(n)
                    step(BLOCKS - 1, parts=2 if side == 0 else 1)

                def stage_targets(side):
                    with v.Fori(0, BLOCKS) as n:
                        v.tensor_copy(stage_i[0][:, :], sx[:, bass.ds(BT * n, BT)]).then_inc(g_row_ok[side], 1)
                        dve.wait_ge(g_sent[side], 16 * BT * (n + 1))
                        v.tensor_copy(rowmax[:, :], eps_t[:, :])

                dense(0, c_bc)
                stage_targets(0)
                v.memset(node_i[:, :], PAD).then_inc(g_pad, 1)
                for q in range(BT):
                    v.tensor_copy(ha[:, q * P:(q + 1) * P], bit_b[:, :])
                dve.wait_ge(g_dst_in, 64)
                encode()
                sort(s_tt[1], s_pt[1])
                decode(s_line)
                prepare(1, sorted_in, spare)
                dve.wait_ge(g_rows_stored, 16)
                dense(1, relub)
                link(v.memset(carry[:, :], 0.0))
                with v.Fori(0, BLOCKS) as n:
                    v.tensor_copy(stage_i[0][:, :], gi[1][:, bass.ds(BT * n, BT)]).then_inc(g_edge, 1)
                    dve.wait_ge(g_x, 16 * BT * (n + 1))
                    for t in range(BT):
                        last = v.bn_stats(stat[0][:, t, :], xg[0][:, t, :])
                    last.then_inc(g_stat, 1)
                    dve.wait_ge(g_stat, n + 1)
                    v.tensor_copy(rowmax[:, :], eps_t[:, :])
                    for t in range(BT):
                        last = v.bn_aggr(mv[0][:, t, :], stat[0][:, t, :])
                    last.then_inc(g_var, 1)
                    dve.wait_ge(g_sd, n + 1)
                    v.reciprocal(rstd[0][:, :], sd[0][:, :]).then_inc(g_rstd, 1)
                    dve.wait_ge(g_rstd, n + 1)
                    v.scalar_tensor_tensor(nmr[0][:, :], mv[0][:, :, 0], -1.0, rstd[0][:, :], ALU.mult, ALU.mult).then_inc(g_norm, 1)
                    dve.wait_ge(g_ht, n + 1)
                    v.tensor_copy(rowmax[:, :], eps_t[:, :])
                    dve.wait_ge(g_c, 16 * (n + 1))
                    v.tensor_tensor_scan(agg[0][0:D, :], c_rows[0][0:D, :], p_g[0][0:D, :], carry[0:D, 0:1],
                                         ALU.mult, ALU.add).then_inc(g_agg, 1)
                    dve.wait_ge(g_agg, n + 1)
                    v.tensor_copy(carry[0:D, :], agg[0][0:D, BLK - 1:BLK]).then_inc(g_carry, 1)
                    dve.wait_ge(g_y, n + 1)
                    v.scalar_tensor_tensor(rec[0][:, :, 0:D], p_m[0][:, :, 0:D], 0.0,
                                           relub[:, :].unsqueeze(1).to_broadcast([P, BT, D]),
                                           ALU.max, ALU.subtract).then_inc(g_rec, 1)
                    dve.wait_ge(g_stored, 16 * (n + 1))
                    v.tensor_copy(rowmax[:, :], eps_t[:, :])
                    dve.wait_ge(g_carry, n + 1)
                    v.tensor_copy(carry_p[:, :], eps_t[:, :])
                stage_targets(1)

        @block.tensor
        def _(pe):
            mm = nc.tensor.matmul
            tr = nc.tensor.transpose
            pe.wait_ge(s_const, 1)
            pe.wait_ge(s_r0, 1)
            mm(p_t[:, 0:D], r0[:, :], w2_s[:, :], start=True, stop=True)
            tr(p_u[0:D, 0:D], w_s[:, :], ident[0:D, 0:D]).then_inc(s_pw, 1)
            pe.wait_ge(s_wts, 1)

            def turn(to, of):
                for q in range(BT):
                    last = tr(to[:, q * P:(q + 1) * P], of[:, q * P:(q + 1) * P], ident[:, :])
                return last

            def turn_columns(to, of):
                for t in range(BT):
                    last = tr(to[:, t * P:(t + 1) * P], of[:, t::BT], ident[:, :])
                return last

            def sum_starts(side, nth):
                pe.wait_ge(s_above, nth)
                for k in range(SPAN):
                    last = mm(p_s[0:1, 256 * side:256 * side + GROUPS], in_group[:, k:k + 1], above[:, k, :],
                              start=k == 0, stop=k == SPAN - 1)
                last.then_inc(s_base, 1)

            def sort_turns(to_turn, turned_by, between):
                for t, which in enumerate(turn_from):
                    pe.wait_ge(to_turn, t + 1)
                    last = turn(p_t, key_tiles[which])
                    if t == 13:
                        last = turn(p_u, hb)
                    last.then_inc(turned_by, 1)
                    between(t)

            pe.wait_ge(s_dplane, 1)
            turn_columns(p_z[0], ds_f)
            turn_columns(p_z[1], dn_f).then_inc(s_dturn, 1)
            sort_turns(s_tt[0], s_pt[0], lambda t: sum_starts(1, 1) if t == 4 else None)
            pe.wait_ge(s_tt[0], 15)
            tr(p_u[0:1, 0:P], rowmax[:, :], ident[:, :]).then_inc(s_pt[0], 1)
            pe.wait_ge(s_tt[0], 16)
            mm(p_u[:, 256:257], pmax[0:1, 0:P], one[0:1, 0:1], start=True, stop=True).then_inc(s_pt[0], 1)
            pe.wait_ge(s_tt[0], 17)
            turn_columns(p_t, gidx_f)
            turn_columns(p_u, sorted_in).then_inc(s_pt[0], 1)
            pe.wait_ge(s_tt[0], 18)
            turn_columns(p_t, spare)
            turn_columns(p_u, ha).then_inc(s_pt[0], 1)
            sum_starts(0, 2)
            pe.wait_ge(s_wrong, 1)
            mm(p_s[0:1, COLS - 1:COLS], wrong1[:, 0:1], one[:, 0:1], start=True, stop=True).then_inc(s_wsum, 1)
            pe.wait_ge(s_fast, 1)
            pe.wait_ge(s_dcols, 1)

            def turn_attr(i, b_):
                pe.wait_ge(tripled[b_], i + 1)
                for t in range(BT):
                    last = tr(p_g[b_][0:96, t::BT],
                              attr3[b_][:, t, :, :].rearrange("p a f -> p (a f)"), ident[:, :])
                last.then_inc(turned[b_], 1)

            def layer1(i, b_):
                pe.wait_ge(feats_ok[b_], i + 1)
                mm(p_z[b_][:, :], w1_s[:, :], feats[b_][:, :], start=True, stop=True).then_inc(z_ok[b_], 1)

            def layer2(i, b_):
                pe.wait_ge(hid_ok[b_], i + 1)
                mm(p_m[b_][:, :, 0:D], one_b[0:3, :], nc3[0:3, :, :], start=True, stop=False)
                for t in range(BT):
                    last = mm(p_m[b_][:, t, 0:D], hid[b_][:, t::BT], w2_s[:, :], start=False, stop=t == BT - 1)
                last.then_inc(m_ok[b_], 1)

            def expand(side, j, b_):
                pe.wait_ge(lo_ok[side][b_], j + 1)
                if not isinstance(j, int) or j > 0:
                    pe.wait_ge(sum_ok[side][b_], j)
                mm(p_e[b_][:, :], one_b[0:3, :], c3[side][0:3, :, :].rearrange("p q d -> p (q d)"), start=True, stop=False)
                parts = (upper_b[b_][:, :, :, :], middle_of(b_), lower_b[b_][:, :, :, :])
                for g in range(2):
                    for h in range(2):
                        for t in range(2):
                            q = (2 * g + h) * 2 + t
                            for a in range(2 + h):
                                at = 512 * a + (256 * h if a < 2 else 0) + P * t
                                for w in range(3):
                                    last = mm(p_e[b_][:, q * D:(q + 1) * D], oneh[b_][:, g, at:at + P],
                                              parts[w][:, g, a, :], start=False, stop=(q == 7 and a == 2 and w == 2))
                last.then_inc(exp_ok[side][b_], 1)

            turn_attr(0, 0)
            turn_attr(0, 1)
            layer1(0, 0)

            def turn_src(i, b_, expand_=True):
                if some(i, b_, -1):
                    layer1(*back(i, b_, -1))
                if some(i, b_, 0):
                    layer2(i, b_)
                if some(i, b_, -2):
                    turn_attr(*back(i, b_, -2))
                if expand_ and some(i, b_, SRC_LAG):
                    expand(0, *back(i, b_, SRC_LAG))

            for n in range(SRC_LAG - 1):
                turn_src(n // 2, n % 2)
            with pe.If(pe.value_load(fast[0:1, 0:1], min_val=0, max_val=1)):
                turn_src(SRC_LAG // 2 - 1, 1)
                turns(nc.tensor, turn_src, SRC_LAG // 2, SRC_LAG)

                def turn_h(i, b_):
                    pe.wait_ge(h_ok[b_], i + 1)
                    pe.sem_inc(pe_blocks, 1)
                    for t in range(BT):
                        last = tr(p_g[b_][0:D, t * P:(t + 1) * P], hn[b_][:, t, :], ident[:, :])
                    last.then_inc(ht_ok[b_], 1)

                def conv(i, b_):
                    pe.wait_ge(hts_ok[b_], i + 1)
                    for t in range(BT):
                        last = mm(p_m[b_][:, t, 0:D], agg[b_][0:D, t * P:(t + 1) * P], wb_s[0:D, :], start=True, stop=True)
                    last.then_inc(y_ok[b_], 1)

                def turn_dst(i, b_):
                    if some(i, b_, 2):
                        conv(*back(i, b_, 2))
                    if some(i, b_, DST_LAG + 1):
                        expand(1, *back(i, b_, DST_LAG + 1))
                    if some(i, b_, 0):
                        turn_h(i, b_)

                turns(nc.tensor, turn_dst, 0, DST_LAG)
            with pe.Else():
                turn_src(SRC_LAG // 2 - 1, 1, expand_=False)
                turns(nc.tensor, lambda i, b_: turn_src(i, b_, expand_=False), SRC_LAG // 2, SRC_LAG)
                sort_turns(s_tt[1], s_pt[1], lambda t: None)
                pe.wait_ge(s_tt[1], 15)
                turn_columns(p_t, gidx_f)
                turn_columns(p_u, sorted_in).then_inc(s_pt[1], 1)
                pe.wait_ge(s_tt[1], 16)
                turn_columns(p_t, spare).then_inc(s_pt[1], 1)
                with nc.tensor.Fori(0, BLOCKS) as n:
                    pe.wait_ge(g_h, n + 1)
                    pe.sem_inc(pe_blocks, 1)
                    for t in range(BT):
                        last = tr(p_g[0][0:D, t::BT], hn[0][:, t, :], ident[:, :])
                    last.then_inc(g_ht, 1)
                    pe.wait_ge(g_agg, n + 1)
                    for t in range(BT):
                        last = mm(p_m[0][:, t, 0:D], agg[0][0:D + 1, t::BT], wb_s[:, :], start=True, stop=True)
                    last.then_inc(g_y, 1)


_INS = ['x', 'src', 'dst', 'edge_attr_32', 'L0_gnn_u', 'L0_gnn_W1', 'L0_gnn_b1', 'L0_gnn_W2', 'L0_gnn_b2',
        'L1_gnn_W', 'L1_gnn_b']


def kernel(**inputs):
    import numpy as _np
    import concourse.bacc as _bacc
    from concourse import mybir as _mybir
    from concourse.bass_utils import run_bass_kernel_spmd as _run

    nc = _bacc.Bacc("TRN2", target_bir_lowering=False, num_devices=1)
    arrays, args = {}, []
    for name in _INS:
        a = _np.ascontiguousarray(inputs[name])
        arrays[f"in_{name}_dram"] = a
        args.append(nc.dram_tensor(f"in_{name}_dram", a.shape, _mybir.dt.from_np(a.dtype), kind="ExternalInput").ap())
    args.append(nc.dram_tensor("out_dram", (ROWS, D), _mybir.dt.float32, kind="ExternalOutput").ap())
    build(nc, *args)
    r = _run(nc, [arrays], core_ids=[0])
    return r.results[0]["out_dram"][:N]
```
